# Optimizing a Trainium2 kernel written in Bass

```python
import numpy as np
import jax
import jax.numpy as jnp

def _softmax(x, axis=-1):
    return jax.nn.softmax(x, axis=axis)

def _gelu(x):
    return jax.nn.gelu(x, approximate=True)

def _silu(x):
    return jax.nn.silu(x)

def _sigmoid(x):
    return jax.nn.sigmoid(x)

def _layernorm(x, axis=-1, eps=1e-05):
    m = jnp.mean(x, axis=axis, keepdims=True)
    v = jnp.var(x, axis=axis, keepdims=True)
    return (x - m) / jnp.sqrt(v + eps)

def _scatter_add(tgt, idx, src, axis=0):
    return tgt.at[idx].add(src)

def _segment_sum(src, seg, n):
    return jax.ops.segment_sum(src, seg, n)
kernel_name = 'mk_seq_postln_d1_jaxref_r2_a62a91'

def setup_inputs(seed: int=0):
    np.random.seed(seed)
    _w = jnp.asarray

    def _L0_attn_setup():
        import jax, jax.numpy as jnp
        import numpy as np
        B, L, H, P = (4, 2048, 512, 128)

        def _bin_op(ei, ej):
            A_i, Bu_i = ei
            A_j, Bu_j = ej
            return (A_j * A_i, A_j * Bu_i + Bu_j)

        def _s5(x, log_real, imag, B_real, B_imag, C_real, C_imag, D, log_Delta):
            Lam = jax.lax.complex(-jnp.exp(log_real), imag)
            B_tilde = jax.lax.complex(B_real, B_imag)
            C_tilde = jax.lax.complex(C_real, C_imag)
            Delta = jnp.exp(log_Delta)
            Lambda_bar = jnp.exp(Lam * Delta)
            Lam_safe = jnp.where(jnp.abs(Lam) < 1e-06, jnp.full_like(Lam, 1e-06), Lam)
            B_bar = ((Lambda_bar - 1.0) / Lam_safe)[:, None] * B_tilde
            Bu = x.astype(jnp.complex64) @ B_bar.T
            La = jnp.broadcast_to(Lambda_bar[None, None, :], Bu.shape)
            _, xs = jax.lax.associative_scan(_bin_op, (La, Bu), axis=1)
            ys = jnp.real(xs @ C_tilde.T) + D * x
            return jax.nn.gelu(ys, approximate=False)
        key = jax.random.key(seed)
        ks = jax.random.split(key, 17)
        std_b = 1.0 / H ** 0.5
        std_c = 1.0 / P ** 0.5
        d = {'x': jax.random.normal(ks[0], (B, L, H), dtype=jnp.float32)}
        for i, pfx in enumerate(['fwd', 'bwd']):
            o = 1 + 8 * i
            d[pfx + '_log_real'] = jax.random.normal(ks[o], (P,)) * 0.5
            d[pfx + '_imag'] = jax.random.normal(ks[o + 1], (P,))
            d[pfx + '_B_real'] = jax.random.normal(ks[o + 2], (P, H)) * std_b
            d[pfx + '_B_imag'] = jax.random.normal(ks[o + 3], (P, H)) * std_b
            d[pfx + '_C_real'] = jax.random.normal(ks[o + 4], (H, P)) * std_c
            d[pfx + '_C_imag'] = jax.random.normal(ks[o + 5], (H, P)) * std_c
            d[pfx + '_D'] = jnp.ones((H,), dtype=jnp.float32)
            d[pfx + '_log_Delta'] = jnp.zeros((P,), dtype=jnp.float32)
        return d
    _L0_attn_in = _L0_attn_setup()

    def _L0_ffn_setup():
        import jax, jax.numpy as jnp
        import numpy as np
        EPS = 1e-05

        @jax.custom_vjp
        def ste_quantize(w):
            scale = jnp.maximum(jnp.mean(jnp.abs(w)), EPS)
            return jnp.clip(jnp.round(w / scale), -1.0, 1.0)

        def _ste_fwd(w):
            return (ste_quantize(w), None)

        def _ste_bwd(_, g):
            return (g,)
        ste_quantize.defvjp(_ste_fwd, _ste_bwd)
        key = jax.random.key(seed)
        k1, k2 = jax.random.split(key)
        x = jax.random.normal(k1, (8, 4096, 512), dtype=jnp.float32)
        weight = jax.random.normal(k2, (512, 512), dtype=jnp.float32) * 0.02
        return {'x': x, 'weight': weight}
    _L0_ffn_in = _L0_ffn_setup()
    _d = {'L0_attn_x': _L0_attn_in['x'], 'L0_attn_fwd_log_real': _L0_attn_in['fwd_log_real'], 'L0_attn_fwd_imag': _L0_attn_in['fwd_imag'], 'L0_attn_fwd_B_real': _L0_attn_in['fwd_B_real'], 'L0_attn_fwd_B_imag': _L0_attn_in['fwd_B_imag'], 'L0_attn_fwd_C_real': _L0_attn_in['fwd_C_real'], 'L0_attn_fwd_C_imag': _L0_attn_in['fwd_C_imag'], 'L0_attn_fwd_D': _L0_attn_in['fwd_D'], 'L0_attn_fwd_log_Delta': _L0_attn_in['fwd_log_Delta'], 'L0_attn_bwd_log_real': _L0_attn_in['bwd_log_real'], 'L0_attn_bwd_imag': _L0_attn_in['bwd_imag'], 'L0_attn_bwd_B_real': _L0_attn_in['bwd_B_real'], 'L0_attn_bwd_B_imag': _L0_attn_in['bwd_B_imag'], 'L0_attn_bwd_C_real': _L0_attn_in['bwd_C_real'], 'L0_attn_bwd_C_imag': _L0_attn_in['bwd_C_imag'], 'L0_attn_bwd_D': _L0_attn_in['bwd_D'], 'L0_attn_bwd_log_Delta': _L0_attn_in['bwd_log_Delta'], 'L0_ffn_weight': _L0_ffn_in['weight']}
    _x0 = _d['L0_attn_x']
    _d['L0_attn_x'] = jax.random.normal(jax.random.fold_in(jax.random.key(seed), 1), (4, 2048, 512), dtype=_x0.dtype)
    del _x0
    return _d

def reference(L0_attn_x, L0_attn_fwd_log_real, L0_attn_fwd_imag, L0_attn_fwd_B_real, L0_attn_fwd_B_imag, L0_attn_fwd_C_real, L0_attn_fwd_C_imag, L0_attn_fwd_D, L0_attn_fwd_log_Delta, L0_attn_bwd_log_real, L0_attn_bwd_imag, L0_attn_bwd_B_real, L0_attn_bwd_B_imag, L0_attn_bwd_C_real, L0_attn_bwd_C_imag, L0_attn_bwd_D, L0_attn_bwd_log_Delta, L0_ffn_weight):

    def _L0_attn_ref(x, fwd_log_real, fwd_imag, fwd_B_real, fwd_B_imag, fwd_C_real, fwd_C_imag, fwd_D, fwd_log_Delta, bwd_log_real, bwd_imag, bwd_B_real, bwd_B_imag, bwd_C_real, bwd_C_imag, bwd_D, bwd_log_Delta):
        import jax, jax.numpy as jnp
        import numpy as np
        B, L, H, P = (4, 2048, 512, 128)

        def _bin_op(ei, ej):
            A_i, Bu_i = ei
            A_j, Bu_j = ej
            return (A_j * A_i, A_j * Bu_i + Bu_j)

        def _s5(x, log_real, imag, B_real, B_imag, C_real, C_imag, D, log_Delta):
            Lam = jax.lax.complex(-jnp.exp(log_real), imag)
            B_tilde = jax.lax.complex(B_real, B_imag)
            C_tilde = jax.lax.complex(C_real, C_imag)
            Delta = jnp.exp(log_Delta)
            Lambda_bar = jnp.exp(Lam * Delta)
            Lam_safe = jnp.where(jnp.abs(Lam) < 1e-06, jnp.full_like(Lam, 1e-06), Lam)
            B_bar = ((Lambda_bar - 1.0) / Lam_safe)[:, None] * B_tilde
            Bu = x.astype(jnp.complex64) @ B_bar.T
            La = jnp.broadcast_to(Lambda_bar[None, None, :], Bu.shape)
            _, xs = jax.lax.associative_scan(_bin_op, (La, Bu), axis=1)
            ys = jnp.real(xs @ C_tilde.T) + D * x
            return jax.nn.gelu(ys, approximate=False)
        y_f = _s5(x, fwd_log_real, fwd_imag, fwd_B_real, fwd_B_imag, fwd_C_real, fwd_C_imag, fwd_D, fwd_log_Delta)
        x_flip = jnp.flip(x, axis=1)
        y_b = _s5(x_flip, bwd_log_real, bwd_imag, bwd_B_real, bwd_B_imag, bwd_C_real, bwd_C_imag, bwd_D, bwd_log_Delta)
        return y_f + jnp.flip(y_b, axis=1)

    def _L0_ffn_ref(x, weight):
        import jax, jax.numpy as jnp
        import numpy as np
        EPS = 1e-05

        @jax.custom_vjp
        def ste_quantize(w):
            scale = jnp.maximum(jnp.mean(jnp.abs(w)), EPS)
            return jnp.clip(jnp.round(w / scale), -1.0, 1.0)

        def _ste_fwd(w):
            return (ste_quantize(w), None)

        def _ste_bwd(_, g):
            return (g,)
        ste_quantize.defvjp(_ste_fwd, _ste_bwd)
        w_ternary = ste_quantize(weight)
        scale = jnp.maximum(jnp.mean(jnp.abs(weight)), EPS)
        return jnp.einsum('bsi,oi->bso', x, w_ternary * scale)
    x = L0_attn_x
    x = _layernorm(x + _L0_attn_ref(x, L0_attn_fwd_log_real, L0_attn_fwd_imag, L0_attn_fwd_B_real, L0_attn_fwd_B_imag, L0_attn_fwd_C_real, L0_attn_fwd_C_imag, L0_attn_fwd_D, L0_attn_fwd_log_Delta, L0_attn_bwd_log_real, L0_attn_bwd_imag, L0_attn_bwd_B_real, L0_attn_bwd_B_imag, L0_attn_bwd_C_real, L0_attn_bwd_C_imag, L0_attn_bwd_D, L0_attn_bwd_log_Delta), axis=-1)
    x = _layernorm(x + _L0_ffn_ref(x, L0_ffn_weight), axis=-1)
    return x

_drawn_inputs = setup_inputs


def setup_inputs(seed=0):
    import zlib

    import numpy as np

    out = dict(_drawn_inputs(seed))
    spreads = {'L0_attn_fwd_D': (1.0, 0.2),
     'L0_attn_fwd_log_Delta': (0.0, 0.1),
     'L0_attn_bwd_D': (1.0, 0.2),
     'L0_attn_bwd_log_Delta': (0.0, 0.1)}
    factors = {}
    for name, (base, spread) in spreads.items():
        noise = np.random.default_rng([zlib.crc32(name.encode()), seed]).standard_normal(out[name].shape)
        drawn = base * np.exp(spread * noise) if base else spread * noise
        out[name] = jnp.asarray(drawn.astype(out[name].dtype))
    for name, factor in factors.items():
        out[name] = (out[name] * factor).astype(out[name].dtype)
    return out
```

```python
import concourse.bass as bass
from concourse import mybir
from contextlib import ExitStack
import numpy as np

P = 128
NB, L, H = 4, 2048, 512
T = 512
NK = L // T
HB = H // P
TB = T // P
EPS = 1e-5
LAM_MIN = 1e-6
MAGIC = 12582912.0
TWO_PI = 2 * np.pi
PI_1 = float(np.float32(6.28125))
PI_2 = float(np.float32(TWO_PI - PI_1))
PI_3 = float(np.float32(TWO_PI - PI_1 - PI_2))
PI_DOWN = float(np.nextafter(np.float32(np.pi), np.float32(0)))
F_, B_ = 0, 1


def build(nc, x_d, bt_d, ct_d, wt_d, d_d, par_d, out_d):
    f32, f32r = mybir.dt.float32, mybir.dt.float32r
    ALU = mybir.AluOpType
    ACT = mybir.ActivationFunctionType
    AX = mybir.AxisListType.X

    ctx = ExitStack()
    with ctx:
        def sb(name, shape, dt=f32):
            return ctx.enter_context(nc.sbuf_tensor(name, [P] + shape, dt))

        def sem(name):
            return ctx.enter_context(nc.semaphore(name))

        x_a = sb("x_a", [HB, T])
        x_hi = sb("x_hi", [HB, T], f32r)
        x_lo = sb("x_lo", [HB, T], f32r)
        x_b = sb("x_b", [HB, T])
        bt_hi = sb("bt_hi", [HB, 4, P], f32r)
        bt_lo = sb("bt_lo", [HB, 4, P], f32r)
        ct_hi = sb("ct_hi", [4, H], f32r)
        ct_lo = sb("ct_lo", [4, H], f32r)
        wc = sb("wc", [HB, H], f32r)
        d_sb = sb("d_sb", [2, HB])
        tab_in = sb("tab_in", [2, 2, T])
        tab_out = sb("tab_out", [2, 2, T])
        v_f = sb("v_f", [NK, 2, T])
        st_b = sb("st_b", [NK, 2, T])
        v_b = sb("v_b", [2, T])
        z = sb("z", [2, T])
        st_f = sb("st_f", [2, T])
        prod = sb("prod", [2, 2, T])
        st_hi = sb("st_hi", [2, 2, T], f32r)
        st_lo = sb("st_lo", [2, 2, T], f32r)
        YR = 4
        y = sb("y", [YR, T])
        s = sb("s", [HB, T])
        s_hi = sb("s_hi", [HB, T], f32r)
        s_lo = sb("s_lo", [HB, T], f32r)
        s_t = sb("s_t", [2, H])
        w = sb("w", [TB, H])
        stats = sb("stats", [TB, 2, 6])
        mean_sum = sb("mean_sum", [TB])
        mean_gap = sb("mean_gap", [TB, 2])
        sq_sum = sb("sq_sum", [TB, 2])
        var_e = sb("var_e", [TB])
        neg_mean = sb("neg_mean", [TB])
        rstd = sb("rstd", [TB])
        shift = sb("shift", [TB])
        ident = sb("ident", [P])
        ones = sb("ones", [P])
        small = sb("small", [64])
        minus_half = sb("minus_half", [TB])
        rho = sb("rho", [2])
        scale = sb("scale", [1])

        pu = ctx.enter_context(nc.psum_tensor("pu", [P, 2, 2, T], f32))
        py = ctx.enter_context(nc.psum_tensor("py", [P, 4, T], f32))

        bt_loaded, ct_loaded, wt_loaded, par_loaded = map(sem, (
            "bt_loaded", "ct_loaded", "wt_loaded", "par_loaded"))
        consts_ready, ident_ready = sem("consts_ready"), sem("ident_ready")
        bt_hi_ready, bt_lo_ready = sem("bt_hi_ready"), sem("bt_lo_ready")
        ct_hi_ready, ct_lo_ready = sem("ct_hi_ready"), sem("ct_lo_ready")
        exps_ready, decay_ready = sem("exps_ready"), sem("decay_ready")
        exponent_ready = sem("exponent_ready")
        phase_ready, sincos_ready = sem("phase_ready"), sem("sincos_ready")
        abs_sums, mean_abs, thresholds = sem("abs_sums"), sem("mean_abs"), sem("thresholds")
        ternary_ready, row_means, wc_ready = sem("ternary_ready"), sem("row_means"), sem("wc_ready")
        setup_step, pool_step = sem("setup_step"), sem("pool_step")
        xa_loaded = sem("xa_loaded")
        x_hi_ready, x_lo_ready = sem("x_hi_ready"), sem("x_lo_ready")
        u_done = sem("u_done")
        in_products = sem("in_products")
        zb_ready, outb_products = sem("zb_ready"), sem("outb_products")
        rotated = sem("rotated")
        xb_loaded = sem("xb_loaded")
        zf_ready, outf_products = sem("zf_ready"), sem("outf_products")
        hi_ready = [sem("stf_hi_ready"), sem("stb_hi_ready")]
        lo_ready = [sem("stf_lo_ready"), sem("stb_lo_ready")]
        y_done, y_read = sem("y_done"), sem("y_read")
        gelu_ready, s_added = sem("gelu_ready"), sem("s_added")
        s_hi_ready, s_lo_ready = sem("s_hi_ready"), sem("s_lo_ready")
        t_done, t_copied = sem("t_done"), sem("t_copied")
        ff_done, w_ready = sem("ff_done"), sem("w_ready")
        stats_ready = sem("stats_ready")
        halves_read, gap_squared, sq_ready = sem("halves_read"), sem("gap_squared"), sem("sq_ready")
        var_ready, rstd_ready, shift_ready = sem("var_ready"), sem("rstd_ready"), sem("shift_ready")
        eps_var = sem("eps_var")
        final_ready, stored = sem("final_ready"), sem("stored")

        def first(b):
            return isinstance(b, int) and b == 0

        def last(b):
            return isinstance(b, int) and b == NB

        def chunk_a(b, k):
            return NK * b + k

        def chunk_b(b, k):
            return NK * (b - 1) + k

        def slot(b, pos):
            return pos + (b % 2) * (NK - 1 - 2 * pos)

        def rotations(b, k):
            if first(b):
                return 3 * k - 1 if k else 0
            if last(b):
                return 3 * NK + 4 * NK * (NB - 1) + (k + 1 if k else 0)
            return 3 * NK + 4 * NK * (b - 1) + 4 * k

        def out_f_done(b, k):
            return rotations(b, k) + (4 if k == NK - 1 else 1 if last(b) and k else 2)

        def start(eng, *sems):
            for x in sems:
                eng.sem_inc(x, 16 if x is stored else 1)

        def steps(eng, step):
            for k in range(NK):
                step(0, k)
            with eng.Fori(1, NB) as b:
                for k in range(NK):
                    step(b, k)
            for k in range(NK):
                step(NB, k)

        bt_raw = s[:, :, :].rearrange("p h (c q) -> p h c q", c=4)
        ct_raw, wt_raw = w[:, :, :], y[:, :, :]
        abs_out, ternary = s[:, :, :], x_b[:, :, :]
        th_hi = sb("th_hi", [2], f32r)

        block = ctx.enter_context(nc.Block())

        @block.sync
        def _(sp):
            sp.dma_start(bt_raw, bt_d).then_inc(bt_loaded, 16)
            sp.dma_start(small[:, 0:6], par_d).then_inc(par_loaded, 16)

            def load_a(c, n):
                sp.dma_start(x_a[:, :, :], x_d[bass.ds(c, 1)].rearrange("o p h t -> p (o h) t"))\
                  .then_inc(xa_loaded, 16)

            def step(b, k):
                if not last(b):
                    if not (first(b) and k == 0):
                        sp.wait_ge(x_lo_ready, HB * chunk_a(b, k))
                    load_a(NK * b + (NK - 1 - k), None)
                if first(b) and k == 0:
                    sp.dma_start(ct_raw, ct_d).then_inc(ct_loaded, 16)
                    sp.dma_start(d_sb[:, :, :], d_d).then_inc(ct_loaded, 16)
                    sp.dma_start(wt_raw, wt_d).then_inc(wt_loaded, 16)
                if first(b) and k == NK - 1:
                    sp.wait_ge(wc_ready, HB)
                    sp.dma_start(x_b[:, :, :], x_d[0]).then_inc(xb_loaded, 16)
                if not first(b) and not (last(b) and k == NK - 1):
                    sp.wait_ge(s_added, 1 + 2 * HB * (chunk_b(b, k) + 1))
                    sp.dma_start(x_b[:, :, :],
                                 x_d[bass.ds(chunk_b(b, k) + 1, 1)].rearrange("o p h t -> p (o h) t"))\
                      .then_inc(xb_loaded, 16)

            steps(sp, step)
            sp.wait_ge(stored, 16 + 16 * NB * NK)

        @block.tensor
        def _(pe):
            start(pe, y_done, ff_done)

            def u_products(b, k):
                for d in (F_, B_):
                    n = 2 * chunk_a(b, k) + d
                    if not (first(b) and k == 0):
                        pe.wait_ge(in_products, n - 1)
                    pe.wait_ge(x_hi_ready, chunk_a(b, k) + 1)
                    if first(b) and k == 0:
                        pe.wait_ge(bt_hi_ready, 1)
                        pe.wait_ge(bt_lo_ready, 1)
                    for c in range(2):
                        acc = pu[:, d, c, :]
                        for h in range(HB):
                            nc.tensor.matmul(acc, bt_lo[:, h, 2 * d + c, :], x_hi[:, h, :],
                                             start=(h == 0), stop=False)
                            mm = nc.tensor.matmul(acc, bt_hi[:, h, 2 * d + c, :], x_hi[:, h, :],
                                                  start=False, stop=False)
                        for h in range(HB):
                            if d == 0 and c == 0:
                                pe.wait_ge(x_lo_ready, HB * chunk_a(b, k) + h + 1)
                            mm = nc.tensor.matmul(acc, bt_hi[:, h, 2 * d + c, :], x_lo[:, h, :],
                                                  start=False, stop=(h == HB - 1))
                    mm.then_inc(u_done, 1)

            def y_products(b, k):
                n = chunk_b(b, k)
                for d in (F_, B_):
                    pe.wait_ge(lo_ready[d], 1 + n + 1)
                    for h in range(HB):
                        j = HB * d + h
                        bank = j % 4
                        if j == 0:
                            pe.wait_ge(w_ready, 1 + TB * n)
                            pe.wait_ge(t_copied, 1 + TB * n)
                        if j >= 4:
                            pe.wait_ge(y_read, 2 * HB * n + j - 3)
                        for c in range(2):
                            hi, lo = ct_hi[:, 2 * d + c, P * h:P * h + P], ct_lo[:, 2 * d + c, P * h:P * h + P]
                            nc.tensor.matmul(py[:, bank, :], lo, st_hi[:, d, c, :],
                                             start=(c == 0), stop=False)
                            nc.tensor.matmul(py[:, bank, :], hi, st_hi[:, d, c, :],
                                             start=False, stop=False)
                            mm = nc.tensor.matmul(py[:, bank, :], hi, st_lo[:, d, c, :],
                                                  start=False, stop=(c == 1))
                        mm.then_inc(y_done, 1)

            def feed_forward(b, k):
                n = chunk_b(b, k)
                pe.wait_ge(y_read, 2 * HB * (n + 1))
                for t in range(TB):
                    cols = slice(P * t, P * t + P)
                    if t >= 2:
                        pe.wait_ge(t_copied, 1 + TB * n + t - 1)
                    if t == 0:
                        pe.wait_ge(s_added, 1 + 2 * HB * (n + 1))
                    for h in range(HB):
                        mm = nc.tensor.transpose(py[:, 2 + t % 2, P * h:P * h + P], s[:, h, cols], ident[:, :])
                    mm.then_inc(t_done, 1)
                    if t >= 2:
                        pe.wait_ge(w_ready, 1 + TB * n + t - 1)
                    if t == 0:
                        pe.wait_ge(s_lo_ready, HB * (n + 1))
                    for h in range(HB):
                        nc.tensor.matmul(py[:, t % 2, :], s_hi[:, h, cols], wc[:, h, :],
                                         start=(h == 0), stop=False)
                    for h in range(HB):
                        mm = nc.tensor.matmul(py[:, t % 2, :], s_lo[:, h, cols], wc[:, h, :],
                                              start=False, stop=(h == HB - 1))
                    mm.then_inc(ff_done, 1)

            def mean_setup():
                pe.wait_ge(abs_sums, 1)
                pe.wait_ge(consts_ready, 1)
                nc.tensor.matmul(py[:, 0, 0:1], ones[:, :], small[:, 40:41], start=True, stop=True)\
                  .then_inc(mean_abs, 1)

            def row_means_setup():
                pe.wait_ge(ternary_ready, 1)
                for h in range(HB):
                    mm = nc.tensor.matmul(py[:, 1, :], ones[:, :], x_b[:, h, :],
                                          start=(h == 0), stop=(h == HB - 1))
                mm.then_inc(row_means, 1)

            def step(b, k):
                if not first(b):
                    y_products(b, k)
                if not last(b):
                    u_products(b, k)
                if not first(b):
                    feed_forward(b, k)
                if first(b) and k == 0:
                    mean_setup()
                if first(b) and k == 2:
                    row_means_setup()
                if first(b) and k == 3:
                    pe.wait_ge(wc_ready, HB)
                    pe.wait_ge(ct_lo_ready, 1)
                    pe.wait_ge(ident_ready, 2)

            steps(pe, step)

        @block.scalar
        def _(act):
            start(act, t_copied, stored)

            act.wait_ge(bt_loaded, 16)
            nc.scalar.activation(bt_hi[:, :, :, :], bt_raw, ACT.Copy).then_inc(bt_hi_ready, 1)

            def ct_setup():
                act.wait_ge(ct_loaded, 32)
                for c in range(4):
                    last_ct = nc.scalar.activation(ct_hi[:, c, :], ct_raw[:, c, :], ACT.Copy,
                                                   scale=(1.0 if c % 2 == 0 else -1.0))
                last_ct.then_inc(ct_hi_ready, 1)
                act.wait_ge(wt_loaded, 16)
                act.wait_ge(bt_lo_ready, 1)
                nc.scalar.activation(abs_out, wt_raw, ACT.Abs, accum_out=small[:, 40:41]).then_inc(abs_sums, 1)

            def split_x(b, k):
                if not (first(b) and k == 0):
                    act.wait_ge(u_done, 2 * chunk_a(b, k))
                act.wait_ge(xa_loaded, 16 * (chunk_a(b, k) + 1))
                nc.scalar.activation(x_hi[:, :, :], x_a[:, :, :], ACT.Copy).then_inc(x_hi_ready, 1)

            def split_f(b, k, done):
                n = chunk_b(b, k)
                act.wait_ge(rotated, done)
                act.wait_ge(y_done, 1 + 2 * HB * n)
                nc.scalar.activation(st_hi[:, F_, :, :], st_f[:, :, :], ACT.Copy).then_inc(hi_ready[F_], 1)

            def split_b(b, k):
                n = chunk_b(b, k)
                if k == 0:
                    act.wait_ge(rotated, rotations(b, 0) + 1)
                act.wait_ge(y_done, 1 + 2 * HB * n)
                nc.scalar.activation(st_hi[:, B_, :, :], st_b[:, bass.ds(slot(b - 1, k), 1), :, :]
                                     .rearrange("p o c t -> p (o c) t"), ACT.Copy).then_inc(hi_ready[B_], 1)

            def step(b, k):
                if not last(b):
                    split_x(b, k)
                if first(b) and k == 0:
                    act.wait_ge(phase_ready, 1)
                    for d in (F_, B_):
                        nc.scalar.activation(tab_out[:, d, 1, :], prod[:, d, 0, :], ACT.Sin)
                        sc = nc.scalar.activation(tab_out[:, d, 0, :], prod[:, d, 1, :], ACT.Sin, scale=-1.0)
                    sc.then_inc(sincos_ready, 1)
                    ct_setup()
                if not first(b):
                    if k == 0:
                        split_b(b, 0)
                    n = chunk_b(b, k)

                    def s_high(h):
                        act.wait_ge(s_added, 1 + 2 * HB * n + HB + h + 1)
                        nc.scalar.activation(s_hi[:, h, :], s[:, h, :], ACT.Copy).then_inc(s_hi_ready, 1)

                    for j in range(2 * HB):
                        act.wait_ge(y_read, 2 * HB * n + j + 1)
                        nc.scalar.activation(y[:, j % YR, :], y[:, j % YR, :], ACT.Gelu).then_inc(gelu_ready, 1)
                        if j >= HB + 1:
                            s_high(j - HB - 1)
                    s_high(HB - 1)
                if not first(b) and not (last(b) and k == NK - 1):
                    nb, nk = (b, k + 1) if k < NK - 1 else (b + 1, 0)
                    split_f(nb, nk, out_f_done(b, k))
                    if nk:
                        split_b(nb, nk)
                if first(b) and k == NK - 1:
                    split_f(1, 0, out_f_done(0, k))
                if not first(b):
                    for t in range(TB):
                        act.wait_ge(t_done, TB * n + t + 1)
                        act.wait_ge(w_ready, 1 + TB * n + max(t - 1, 0))
                        nc.scalar.activation(s_t[:, t % 2, :], py[:, 2 + t % 2, :], ACT.Copy)\
                          .then_inc(t_copied, 1)
                    act.wait_ge(shift_ready, n + 1)
                    for t in range(TB):
                        fin = nc.scalar.activation(w[:, t, :], w[:, t, :], ACT.Identity,
                                                   bias=shift[:, t:t + 1], scale=rstd[:, t:t + 1])
                    fin.then_inc(final_ready, 1)
                    act.wait_ge(final_ready, n + 1)
                    act.dma_start(out_d[bass.ds(n, 1)].rearrange("o (t p) h -> p (o t) h", p=P), w[:, :, :])\
                       .then_inc(stored, 16)

            steps(act, step)

        @block.gpsimd
        def _(pool):
            start(pool, s_added, lo_ready[F_], lo_ready[B_])

            count = [0]

            def link(ins):
                count[0] += 1
                ins.then_inc(pool_step, 1)
                pool.wait_ge(pool_step, count[0])

            nc.gpsimd.memset(minus_half[:, :], -0.5)
            link(nc.gpsimd.memset(small[:, 44:48], float(np.e)))
            pool.wait_ge(par_loaded, 16)
            nc.gpsimd.tensor_tensor(small[:, 8:12], small[:, 44:48], small[:, 0:4], ALU.pow).then_inc(exps_ready, 1)
            nc.gpsimd.memset(ones[:, :], 1.0 / H).then_inc(consts_ready, 1)
            nc.gpsimd.memset(ident[:, :], 0.0).then_inc(ident_ready, 1)
            pool.wait_ge(ident_ready, 1)
            nc.gpsimd.affine_select(out=ident[:, :], in_=ident[:, :], compare_op=ALU.not_equal, fill=1.0,
                                    base=0, pattern=[[-1, P]], channel_multiplier=1).then_inc(ident_ready, 1)
            pool.wait_ge(exponent_ready, 1)
            nc.gpsimd.tensor_tensor(rho[:, :], small[:, 44:46], small[:, 12:14], ALU.pow).then_inc(decay_ready, 1)

            def ct_setup():
                pool.wait_ge(ct_hi_ready, 1)
                for c in range(4):
                    if c % 2 == 0:
                        op = nc.gpsimd.tensor_tensor(ct_lo[:, c, :], ct_raw[:, c, :], ct_hi[:, c, :].bitcast(f32), ALU.subtract)
                    else:
                        link(nc.gpsimd.tensor_scalar(ct_raw[:, c, :], ct_raw[:, c, :], -1.0, None, ALU.mult))
                        op = nc.gpsimd.tensor_tensor(ct_lo[:, c, :], ct_raw[:, c, :], ct_hi[:, c, :].bitcast(f32), ALU.subtract)
                op.then_inc(ct_lo_ready, 1)

            def ternary_setup():
                pool.wait_ge(thresholds, 1)
                link(nc.gpsimd.tensor_scalar(x_b[:, :, :], wt_raw, small[:, 41:42], None, ALU.is_gt))
                link(nc.gpsimd.tensor_scalar(wt_raw, wt_raw, small[:, 42:43], None, ALU.is_lt))
                nc.gpsimd.tensor_tensor(x_b[:, :, :], x_b[:, :, :], wt_raw, ALU.subtract).then_inc(ternary_ready, 1)

            def x_low(b, k, h):
                if h == 0:
                    pool.wait_ge(x_hi_ready, chunk_a(b, k) + 1)
                nc.gpsimd.tensor_tensor(x_lo[:, h, :], x_a[:, h, :], x_hi[:, h, :].bitcast(f32), ALU.subtract)\
                  .then_inc(x_lo_ready, 1)

            def state_low(d, src, n):
                pool.wait_ge(hi_ready[d], n + 1)
                nc.gpsimd.tensor_tensor(st_lo[:, d, :, :], src, st_hi[:, d, :, :].bitcast(f32), ALU.subtract)\
                  .then_inc(lo_ready[d], 1)

            def split_b(b, k):
                state_low(B_, st_b[:, bass.ds(slot(b - 1, k), 1), :, :].rearrange("p o c t -> p (o c) t"),
                          chunk_b(b, k))

            def step(b, k):
                n = None if first(b) else chunk_b(b, k)
                if not first(b) and k == 0:
                    split_b(b, 0)
                if not last(b) and first(b):
                    for h in range(HB):
                        x_low(b, k, h)
                if first(b) and k == 0:
                    ct_setup()
                if first(b) and k == 1:
                    ternary_setup()
                if not first(b):
                    pool.wait_ge(xb_loaded, 16 * (n + 1))
                    pool.wait_ge(ff_done, 1 + TB * n)

                    def s_low(h):
                        pool.wait_ge(s_hi_ready, HB * n + h + 1)
                        nc.gpsimd.tensor_tensor(s_lo[:, h, :], s[:, h, :], s_hi[:, h, :].bitcast(f32),
                                                ALU.subtract).then_inc(s_lo_ready, 1)

                    for j in range(2 * HB):
                        h = j % HB
                        if not last(b) and j < HB:
                            x_low(b, k, j)
                        pool.wait_ge(gelu_ready, 2 * HB * n + j + 1)
                        nc.gpsimd.tensor_tensor(s[:, h, :], (x_b if j < HB else s)[:, h, :], y[:, j % YR, :],
                                                ALU.add).then_inc(s_added, 1)
                        if j >= HB + 2:
                            s_low(j - HB - 2)
                    s_low(HB - 2)
                    s_low(HB - 1)
                if not first(b) and not (last(b) and k == NK - 1):
                    nb, nk = (b, k + 1) if k < NK - 1 else (b + 1, 0)
                    state_low(F_, st_f[:, :, :], chunk_b(nb, nk))
                    if nk:
                        split_b(nb, nk)
                if first(b) and k == NK - 1:
                    state_low(F_, st_f[:, :, :], 0)
                if not first(b):
                    pool.wait_ge(var_ready, n + 1)
                    nc.gpsimd.tensor_tensor(rstd[:, :], var_e[:, :], minus_half[:, :], ALU.pow).then_inc(rstd_ready, 1)
                    pool.wait_ge(rstd_ready, n + 1)
                    nc.gpsimd.tensor_tensor(shift[:, :], neg_mean[:, :], rstd[:, :], ALU.mult).then_inc(shift_ready, 1)

            steps(pool, step)

        @block.vector
        def _(dve):
            start(dve, w_ready)

            count = [0]

            def link(ins):
                count[0] += 1
                ins.then_inc(setup_step, 1)
                dve.wait_ge(setup_step, count[0])

            V = nc.vector

            def tables_setup():
                jv = z
                link(V.memset(st_f[:, 0, :], 1.0))
                link(V.tensor_tensor_scan(jv[:, 0, :], st_f[:, 0, :], st_f[:, 0, :], 0.0, ALU.mult, ALU.add))
                link(V.tensor_copy(jv[:, 1, ::-1], jv[:, 0, :]))
                dve.wait_ge(exps_ready, 1)
                delta, theta = small[:, 10:12], small[:, 14:16]
                link(V.scalar_tensor_tensor(out=small[:, 12:14], in0=small[:, 8:10], scalar=-1.0, in1=delta,
                                            op0=ALU.mult, op1=ALU.mult))
                V.tensor_tensor(theta, small[:, 4:6], delta, ALU.mult).then_inc(exponent_ready, 1)
                dve.wait_ge(exponent_ready, 1)
                turns, th_lo = small[:, 16:18], small[:, 20:22]
                link(V.tensor_scalar(turns, theta, 1 / TWO_PI, MAGIC, ALU.mult, ALU.add))
                link(V.tensor_scalar(turns, turns, MAGIC, None, ALU.subtract))
                for part in (PI_1, PI_2, PI_3):
                    link(V.scalar_tensor_tensor(out=theta, in0=turns, scalar=-part, in1=theta,
                                                op0=ALU.mult, op1=ALU.add))
                link(V.tensor_copy(th_hi[:, :], theta))
                link(V.tensor_tensor(th_lo, theta, th_hi[:, :].bitcast(f32), ALU.subtract))
                for d in (F_, B_):
                    ph, q = prod[:, d, 0, :], prod[:, d, 1, :]
                    link(V.tensor_scalar(ph, jv[:, d, :], th_hi[:, d:d + 1].bitcast(f32), None, ALU.mult))
                    link(V.tensor_scalar(q, jv[:, d, :], theta[:, d:d + 1], 1 / TWO_PI, ALU.mult, ALU.mult))
                    link(V.tensor_scalar(q, q, MAGIC, MAGIC, ALU.add, ALU.subtract))
                    link(V.scalar_tensor_tensor(out=ph, in0=q, scalar=-PI_1, in1=ph, op0=ALU.mult, op1=ALU.add))
                    link(V.scalar_tensor_tensor(out=ph, in0=q, scalar=-PI_2, in1=ph, op0=ALU.mult, op1=ALU.add))
                    link(V.scalar_tensor_tensor(out=ph, in0=jv[:, d, :], scalar=th_lo[:, d:d + 1], in1=ph,
                                                op0=ALU.mult, op1=ALU.add))
                    link(V.tensor_scalar(ph, ph, PI_DOWN, -PI_DOWN, ALU.min, ALU.max))
                    link(V.scalar_tensor_tensor(out=q, in0=ph, scalar=-1.0, in1=ph, op0=ALU.mult, op1=ALU.max))
                    op = V.tensor_scalar(q, q, float(np.pi / 2), None, ALU.subtract)
                op.then_inc(phase_ready, 1)
                a, b_, m, keep = small[:, 22:24], small[:, 4:6], small[:, 24:26], small[:, 26:28]
                link(V.tensor_tensor(a, small[:, 8:10], small[:, 8:10], ALU.mult))
                link(V.tensor_tensor(m, b_, b_, ALU.mult))
                link(V.tensor_tensor(m, m, a, ALU.add))
                link(V.tensor_scalar(m, m, LAM_MIN ** 2, None, ALU.is_lt))
                link(V.tensor_scalar(keep, m, -1.0, 1.0, ALU.mult, ALU.add))
                link(V.tensor_scalar(m, m, LAM_MIN, None, ALU.mult))
                link(V.scalar_tensor_tensor(out=a, in0=small[:, 8:10], scalar=-1.0, in1=keep,
                                            op0=ALU.mult, op1=ALU.mult))
                link(V.tensor_tensor(a, a, m, ALU.add))
                bb = small[:, 28:30]
                link(V.tensor_tensor(bb, b_, keep, ALU.mult))
                den, t0 = small[:, 30:32], small[:, 32:34]
                link(V.tensor_tensor(den, a, a, ALU.mult))
                link(V.tensor_tensor(t0, bb, bb, ALU.mult))
                link(V.tensor_tensor(den, den, t0, ALU.add))
                link(V.reciprocal(den, den))
                dve.wait_ge(sincos_ready, 1)
                dve.wait_ge(decay_ready, 1)
                lr, li, g = small[:, 34:36], small[:, 36:38], small[:, 48:52]
                for d, j in ((F_, 0), (B_, T - 1)):
                    link(V.tensor_tensor(lr[:, d:d + 1], tab_out[:, d, 0, j:j + 1], rho[:, d:d + 1], ALU.mult))
                    link(V.tensor_tensor(li[:, d:d + 1], tab_out[:, d, 1, j:j + 1], rho[:, d:d + 1], ALU.mult))
                link(V.tensor_scalar(lr, lr, -1.0, None, ALU.add))
                link(V.tensor_tensor(g[:, 0:2], lr, a, ALU.mult))
                link(V.tensor_tensor(t0, li, bb, ALU.mult))
                link(V.tensor_tensor(g[:, 0:2], g[:, 0:2], t0, ALU.add))
                link(V.tensor_tensor(g[:, 2:4], li, a, ALU.mult))
                link(V.tensor_tensor(t0, lr, bb, ALU.mult))
                link(V.tensor_tensor(g[:, 2:4], g[:, 2:4], t0, ALU.subtract))
                link(V.tensor_tensor(g[:, 0:2], g[:, 0:2], den, ALU.mult))
                link(V.tensor_tensor(g[:, 2:4], g[:, 2:4], den, ALU.mult))
                for d in (F_, B_):
                    gr, gi = g[:, d:d + 1], g[:, 2 + d:3 + d]
                    cos, sin = tab_out[:, d, 0, :], tab_out[:, d, 1, :]
                    link(V.tensor_scalar(prod[:, 0, 0, :], sin, gi, None, ALU.mult))
                    link(V.tensor_scalar(prod[:, 0, 1, :], sin, gr, None, ALU.mult))
                    link(V.scalar_tensor_tensor(out=tab_in[:, d, 0, :], in0=cos, scalar=gr, in1=prod[:, 0, 0, :],
                                                op0=ALU.mult, op1=ALU.add))
                    link(V.scalar_tensor_tensor(out=tab_in[:, d, 1, :], in0=cos, scalar=gi, in1=prod[:, 0, 1, :],
                                                op0=ALU.mult, op1=ALU.subtract))

            def ternary_setup():
                dve.wait_ge(mean_abs, 1)
                link(V.tensor_scalar(scale[:, :], py[:, 0, 0:1], 1.0 / H, EPS, ALU.mult, ALU.max))
                link(V.tensor_scalar(small[:, 41:42], scale[:, :], 0.5, None, ALU.mult))
                V.tensor_scalar(small[:, 42:43], scale[:, :], -0.5, None, ALU.mult).then_inc(thresholds, 1)

            def centre_setup():
                dve.wait_ge(row_means, 1)
                for h in range(HB):
                    V.tensor_tensor(wc[:, h, :], x_b[:, h, :], py[:, 1, :], ALU.subtract).then_inc(wc_ready, 1)

            def wide(table):
                return table.to_broadcast([P, 2, T])

            def rotate_in(b, k, d, done):
                n = 2 * chunk_a(b, k) + d
                dve.wait_ge(rotated, done)
                dve.wait_ge(u_done, n + 1)
                V.tensor_tensor(prod[:, 0, :, :], pu[:, d, :, :], wide(tab_in[:, d, 0:1, :]), ALU.mult)
                V.tensor_tensor(prod[:, 1, :, :], pu[:, d, :, :], wide(tab_in[:, d, 1:2, :]), ALU.mult)\
                 .then_inc(in_products, 1)
                dve.wait_ge(in_products, n + 1)
                if d == F_:
                    sl = bass.ds(slot(b, NK - 1 - k), 1)
                    re, im = v_f[:, sl, 0, :], v_f[:, sl, 1, :]
                    re, im = (v.rearrange("p o t -> p (o t)") for v in (re, im))
                else:
                    re, im = v_b[:, 0, :], v_b[:, 1, :]
                V.tensor_tensor(re, prod[:, 0, 0, :], prod[:, 1, 1, :], ALU.subtract)
                V.tensor_tensor(im, prod[:, 0, 1, :], prod[:, 1, 0, :], ALU.add).then_inc(rotated, 1)

            def rotate_out(n, d, re, im, z_ready, products):
                dve.wait_ge(z_ready, n + 1)
                V.tensor_tensor(prod[:, 0, :, :], z[:, :, :], wide(tab_out[:, d, 0:1, :]), ALU.mult)
                V.tensor_tensor(prod[:, 1, :, :], z[:, :, :], wide(tab_out[:, d, 1:2, :]), ALU.mult)\
                 .then_inc(products, 1)
                dve.wait_ge(products, n + 1)
                V.tensor_tensor(re, prod[:, 0, 0, :], prod[:, 1, 1, :], ALU.subtract)
                V.tensor_tensor(im, prod[:, 0, 1, :], prod[:, 1, 0, :], ALU.add).then_inc(rotated, 1)

            def scan_b(b, k, c, done):
                dve.wait_ge(rotated, done)
                if k == 0:
                    init = 0.0
                else:
                    init = st_b[:, bass.ds(slot(b, NK - k), 1), c, 0:1].rearrange("p o t -> p (o t)")
                op = V.tensor_tensor_scan(z[:, c, ::-1], rho[:, B_:B_ + 1].to_broadcast([P, T]), v_b[:, c, ::-1],
                                          init, ALU.mult, ALU.add)
                if c:
                    op.then_inc(zb_ready, 1)

            def out_b(b, k):
                sl = bass.ds(slot(b, NK - 1 - k), 1)
                re, im = (st_b[:, sl, c, :].rearrange("p o t -> p (o t)") for c in range(2))
                if not first(b):
                    dve.wait_ge(lo_ready[B_], 1 + chunk_b(b, k) + 1)
                rotate_out(chunk_a(b, k), B_, re, im, zb_ready, outb_products)

            def scan_f(b, k, c, done):
                dve.wait_ge(rotated, done)
                if k == 0:
                    init = 0.0
                else:
                    init = st_f[:, c, T - 1:T]
                sl = bass.ds(slot(b - 1, k), 1)
                op = V.tensor_tensor_scan(z[:, c, :], rho[:, F_:F_ + 1].to_broadcast([P, T]),
                                          v_f[:, sl, c, :].rearrange("p o t -> p (o t)"), init, ALU.mult, ALU.add)
                if c:
                    op.then_inc(zf_ready, 1)

            def out_f(b, k):
                n = chunk_b(b, k)
                dve.wait_ge(lo_ready[F_], 1 + n)
                rotate_out(n, F_, st_f[:, 0, :], st_f[:, 1, :], zf_ready, outf_products)

            def read_y(b, k, j):
                n = chunk_b(b, k)
                d, h = divmod(j, HB)
                if j == 0:
                    dve.wait_ge(xb_loaded, 16 * (n + 1))
                if j >= YR:
                    dve.wait_ge(s_added, 1 + 2 * HB * n + j - YR + 1)
                elif j == 0:
                    dve.wait_ge(s_added, 1 + 2 * HB * n)
                dve.wait_ge(y_done, 1 + 2 * HB * n + j + 1)
                V.scalar_tensor_tensor(out=y[:, j % YR, :], in0=x_b[:, h, :], scalar=d_sb[:, d, h:h + 1],
                                       in1=py[:, j % 4, :], op0=ALU.mult, op1=ALU.add).then_inc(y_read, 1)

            def norm(b, k):
                n = chunk_b(b, k)
                dve.wait_ge(stored, 16 + 16 * n)
                for t in range(TB):
                    dve.wait_ge(t_copied, 1 + TB * n + t + 1)
                    V.bn_stats(stats[:, t, 0, :], s_t[:, t % 2, :]).then_inc(stats_ready, 1)
                    dve.wait_ge(ff_done, 1 + TB * n + t + 1)
                    V.scalar_tensor_tensor(out=w[:, t, :], in0=py[:, t % 2, :], scalar=scale[:, 0:1],
                                           in1=s_t[:, t % 2, :], op0=ALU.mult, op1=ALU.add).then_inc(w_ready, 1)
                    dve.wait_ge(w_ready, 1 + TB * n + t + 1)
                    V.bn_stats(stats[:, t, 1, :], w[:, t, :]).then_inc(stats_ready, 1)
                dve.wait_ge(stats_ready, 2 * TB * (n + 1))
                V.tensor_tensor(mean_sum[:, :], stats[:, :, 1, 1], stats[:, :, 1, 4], ALU.add)
                V.tensor_tensor(sq_sum[:, :, :], stats[:, :, :, 2], stats[:, :, :, 5], ALU.add)
                V.tensor_tensor(mean_gap[:, :, :], stats[:, :, :, 1], stats[:, :, :, 4], ALU.subtract)\
                 .then_inc(halves_read, 1)
                dve.wait_ge(halves_read, n + 1)
                V.tensor_tensor(mean_gap[:, :, :], mean_gap[:, :, :], mean_gap[:, :, :], ALU.mult)\
                 .then_inc(gap_squared, 1)
                V.tensor_scalar(neg_mean[:, :], mean_sum[:, :], -0.5, None, ALU.mult)
                dve.wait_ge(gap_squared, n + 1)
                V.scalar_tensor_tensor(out=sq_sum[:, :, :], in0=mean_gap[:, :, :], scalar=H / 4, in1=sq_sum[:, :, :],
                                       op0=ALU.mult, op1=ALU.add).then_inc(sq_ready, 1)
                dve.wait_ge(sq_ready, n + 1)
                V.scalar_tensor_tensor(out=var_e[:, :], in0=sq_sum[:, :, 0], scalar=EPS, in1=sq_sum[:, :, 1],
                                       op0=ALU.mult, op1=ALU.add).then_inc(eps_var, 1)
                dve.wait_ge(eps_var, n + 1)
                V.tensor_scalar(var_e[:, :], var_e[:, :], 1 / H, EPS * EPS, ALU.mult, ALU.add).then_inc(var_ready, 1)

            def step(b, k):
                prev = None if first(b) and k == 0 else ((b, k - 1) if k else (b - 1, NK - 1))
                if last(b) and k:
                    prev = None
                fill = []
                done = rotations(b, k)
                if prev:
                    fill = [lambda: scan_b(*prev, 0, done), lambda: scan_b(*prev, 1, done), lambda: out_b(*prev)]
                if not first(b):
                    for j in range(2 * HB):
                        read_y(b, k, j)
                        if fill:
                            fill.pop(0)()
                while fill:
                    fill.pop(0)()
                if first(b) and k == 1:
                    ternary_setup()
                if first(b) and k == 3:
                    centre_setup()
                def next_forward():
                    nb, nk = (b, k + 1) if k < NK - 1 else (b + 1, 0)
                    before = out_f_done(b, k) - 1
                    scan_f(nb, nk, 0, before)
                    scan_f(nb, nk, 1, before)
                    out_f(nb, nk)

                if not first(b) and k < NK - 1:
                    next_forward()
                if not last(b):
                    if prev:
                        done = done + 1
                    if not first(b) and k < NK - 1:
                        done = done + 1
                    rotate_in(b, k, F_, done)
                    rotate_in(b, k, B_, done + 1)
                    if k == NK - 1:
                        next_forward()
                if not first(b):
                    norm(b, k)

            dve.wait_ge(bt_hi_ready, 1)
            V.tensor_tensor(bt_lo[:, :, :, :], bt_raw, bt_hi[:, :, :, :].bitcast(f32), ALU.subtract).then_inc(bt_lo_ready, 1)
            tables_setup()
            steps(dve, step)


def kernel(**inputs):
    import numpy as _np
    import concourse.bacc as _bacc
    from concourse import mybir as _mybir
    from concourse.bass_utils import run_bass_kernel_spmd as _run

    a = {n.removeprefix("L0_").removeprefix("attn_"): _np.asarray(v) for n, v in inputs.items()}
    arrays = {
        "x": a["x"].reshape(NB * NK, T, HB, P).transpose(0, 3, 2, 1),
        "bt": _np.stack([a[f"{d}_B_{c}"].T.reshape(HB, P, P) for d in ("fwd", "bwd")
                         for c in ("real", "imag")], 2).transpose(1, 0, 2, 3),
        "ct": _np.stack([a[f"{d}_C_{c}"].T for d in ("fwd", "bwd") for c in ("real", "imag")], 1),
        "wt": a["ffn_weight"].T.reshape(HB, P, H).transpose(1, 0, 2),
        "d": _np.stack([a["fwd_D"].reshape(HB, P).T, a["bwd_D"].reshape(HB, P).T], 1),
        "par": _np.stack([a["fwd_log_real"], a["bwd_log_real"], a["fwd_log_Delta"], a["bwd_log_Delta"],
                          a["fwd_imag"], a["bwd_imag"]], 1),
    }
    arrays = {n: _np.ascontiguousarray(v) for n, v in arrays.items()}
    nc = _bacc.Bacc("TRN2", target_bir_lowering=False, num_devices=1)
    args = [nc.dram_tensor(n, v.shape, _mybir.dt.from_np(v.dtype), kind="ExternalInput").ap()
            for n, v in arrays.items()]
    out = nc.dram_tensor("out", (NB * NK, T, H), _mybir.dt.float32, kind="ExternalOutput").ap()
    build(nc, *args, out)
    r = _run(nc, [arrays], core_ids=[0])
    return r.results[0]["out"].reshape(NB, L, H)
```

```python
import concourse.bass as bass
from concourse import mybir
from contextlib import ExitStack
import numpy as np

P = 128
NB, L, H = 4, 2048, 512
T = 512
NK = L // T
HB = H // P
TB = T // P
EPS = 1e-5
LAM_MIN = 1e-6
MAGIC = 12582912.0
TWO_PI = 2 * np.pi
PI_1 = float(np.float32(6.28125))
PI_2 = float(np.float32(TWO_PI - PI_1))
PI_3 = float(np.float32(TWO_PI - PI_1 - PI_2))
PI_DOWN = float(np.nextafter(np.float32(np.pi), np.float32(0)))
F_, B_ = 0, 1


def build(nc, x_d, bt_d, ct_d, wt_d, d_d, par_d, out_d):
    f32, f32r = mybir.dt.float32, mybir.dt.float32r
    ALU = mybir.AluOpType
    ACT = mybir.ActivationFunctionType
    AX = mybir.AxisListType.X

    ctx = ExitStack()
    with ctx:
        def sb(name, shape, dt=f32):
            return ctx.enter_context(nc.sbuf_tensor(name, [P] + shape, dt))

        def sem(name):
            return ctx.enter_context(nc.semaphore(name))

        x_a = sb("x_a", [HB, T])
        x_hi = sb("x_hi", [2, HB, T], f32r)
        x_lo = sb("x_lo", [2, HB, T], f32r)
        x_b = sb("x_b", [HB, T])
        bt_hi = sb("bt_hi", [HB, 4, P], f32r)
        bt_lo = sb("bt_lo", [HB, 4, P], f32r)
        ct = sb("ct", [4, H])
        wc = sb("wc", [HB, H], f32r)
        d_sb = sb("d_sb", [2, HB])
        tab_in = sb("tab_in", [2, 2, T])
        tab_out = sb("tab_out", [2, 2, T])
        v_f = sb("v_f", [NK, 2, T])
        st_b = sb("st_b", [NK, 2, T])
        v_b = sb("v_b", [2, T])
        z = sb("z", [2, T])
        st_f = sb("st_f", [2, T])
        prod = sb("prod", [2, 2, T])
        y = sb("y", [2 * HB, T])
        s = sb("s", [HB, T])
        s_hi = sb("s_hi", [HB, T], f32r)
        s_lo = sb("s_lo", [HB, T], f32r)
        s_t = sb("s_t", [2, H])
        w = sb("w", [TB, H])
        sums = sb("sums", [2, TB])
        stats = sb("stats", [TB, 6])
        mean_sum = sb("mean_sum", [TB])
        mean_gap = sb("mean_gap", [TB])
        sq_sum = sb("sq_sum", [TB])
        gap_sq = sb("gap_sq", [TB])
        mean_sq = sb("mean_sq", [TB])
        var_e = sb("var_e", [TB])
        neg_mean = sb("neg_mean", [TB])
        rstd = sb("rstd", [TB])
        shift = sb("shift", [TB])
        ident = sb("ident", [P])
        ones = sb("ones", [P])
        small = sb("small", [64])
        minus_half = sb("minus_half", [TB])
        rho = sb("rho", [2])
        scale = sb("scale", [1])

        pu = ctx.enter_context(nc.psum_tensor("pu", [P, 2, 2, T], f32))
        py = ctx.enter_context(nc.psum_tensor("py", [P, 4, T], f32))

        bt_loaded, ct_loaded, wt_loaded, par_loaded = map(sem, (
            "bt_loaded", "ct_loaded", "wt_loaded", "par_loaded"))
        consts_ready, ident_ready = sem("consts_ready"), sem("ident_ready")
        bt_hi_ready, bt_lo_ready = sem("bt_hi_ready"), sem("bt_lo_ready")
        ct_ready = sem("ct_ready")
        exps_ready, decay_ready, theta_ready = sem("exps_ready"), sem("decay_ready"), sem("theta_ready")
        first_sincos, modulus_ready, inverse_ready = map(sem, ("first_sincos", "modulus_ready", "inverse_ready"))
        gain_ready, table_products = sem("gain_ready"), sem("table_products")
        exponent_ready = sem("exponent_ready")
        phase_ready, sincos_ready = sem("phase_ready"), sem("sincos_ready")
        abs_sums, mean_abs, thresholds = sem("abs_sums"), sem("mean_abs"), sem("thresholds")
        ternary_ready, row_means, wc_ready = sem("ternary_ready"), sem("row_means"), sem("wc_ready")
        means_copied = sem("means_copied")
        setup_step, pool_step = sem("setup_step"), sem("pool_step")
        xa_loaded = sem("xa_loaded")
        x_hi_ready, x_lo_ready = sem("x_hi_ready"), sem("x_lo_ready")
        u_done = sem("u_done")
        in_products = sem("in_products")
        zb_ready, outb_products = sem("zb_ready"), sem("outb_products")
        rotated = sem("rotated")
        xb_loaded = sem("xb_loaded")
        zf_ready, outf_products = sem("zf_ready"), sem("outf_products")
        y_done, y_read = sem("y_done"), sem("y_read")
        gelu_ready, s_added = sem("gelu_ready"), sem("s_added")
        s_hi_ready, s_lo_ready = sem("s_hi_ready"), sem("s_lo_ready")
        t_done, t_copied, t_squared = sem("t_done"), sem("t_copied"), sem("t_squared")
        ff_done, w_ready = sem("ff_done"), sem("w_ready")
        stats_ready = sem("stats_ready")
        halves_read, gap_squared, sq_ready = sem("halves_read"), sem("gap_squared"), sem("sq_ready")
        var_ready, rstd_ready, shift_ready = sem("var_ready"), sem("rstd_ready"), sem("shift_ready")
        eps_var = sem("eps_var")
        final_ready, stored = sem("final_ready"), sem("stored")

        def first(b):
            return isinstance(b, int) and b == 0

        def last(b):
            return isinstance(b, int) and b == NB

        def chunk_a(b, k):
            return NK * b + k

        def chunk_b(b, k):
            return NK * (b - 1) + k

        def ahead(b, k):
            return last(b) and 0 < k < NK

        def outputs(b, k):
            here = range(HB if ahead(b, k) else 0, 2 * HB)
            return here, range(HB if ahead(b, k + 1) else 0)

        def following(b, k):
            return (b, k + 1) if k < NK - 1 else (b + 1, 0)

        def slot(b, pos):
            return pos + (b % 2) * (NK - 1 - 2 * pos)

        def rotations(b, k):
            if first(b):
                return 3 * k - 1 if k else 0
            begun = 3 * NK + 1 + 4 * NK * (b - 1)
            if last(b):
                return begun + k
            return begun + (4 * k - 1 if k else 0)

        def out_f_done(b, k):
            return rotations(b, k) + (3 if k == NK - 1 else 1 if last(b) or k == 0 else 2)

        def start(eng, *sems):
            for x in sems:
                eng.sem_inc(x, 16 if x is stored else 1)

        def steps(eng, step):
            for k in range(NK):
                step(0, k)
            with eng.Fori(1, NB) as b:
                for k in range(NK):
                    step(b, k)
            for k in range(NK):
                step(NB, k)

        bt_raw = s[:, :, :].rearrange("p h (c q) -> p h c q", c=4)
        wt_raw = y[:, 0:HB, :]
        ternary = w[:, :, :]
        phase = y[:, HB:2 * HB, :].rearrange("p (d c) t -> p d c t", d=2)
        means = y[:, HB, :]
        th_hi = sb("th_hi", [2], f32r)

        lam_re, is_small, keep, lam_im = small[:, 22:24], small[:, 24:26], small[:, 26:28], small[:, 28:30]
        modulus, temp = small[:, 30:32], small[:, 32:34]
        lr, li, gain = small[:, 34:36], small[:, 36:38], small[:, 48:52]

        block = ctx.enter_context(nc.Block())

        @block.sync
        def _(sp):
            sp.dma_start(small[:, 0:6], par_d).then_inc(par_loaded, 16)
            sp.dma_start(bt_raw, bt_d).then_inc(bt_loaded, 16)

            def load_a(b, k):
                if not (first(b) and k == 0):
                    sp.wait_ge(x_lo_ready, HB * chunk_a(b, k))
                sp.dma_start(x_a[:, :, :], x_d[bass.ds((NK * b) % (NK * NB) + (NK - 1 - k), 1)]
                             .rearrange("o p h t -> p (o h) t")).then_inc(xa_loaded, 16)

            load_a(0, 0)

            def step(b, k):
                if first(b) and k == 0:
                    sp.dma_start(wt_raw, wt_d).then_inc(wt_loaded, 16)
                    sp.dma_start(ct[:, :, :], ct_d).then_inc(ct_loaded, 16)
                    sp.dma_start(d_sb[:, :, :], d_d).then_inc(ct_loaded, 16)
                if not last(b):
                    load_a(*following(b, k))
                if first(b) and k == NK - 1:
                    sp.dma_start(x_b[:, :, :], x_d[0]).then_inc(xb_loaded, 16)
                if not first(b) and not (last(b) and k == NK - 1):
                    if last(b):
                        sp.wait_ge(y_read, 2 * HB * (chunk_b(b, k) + 1))
                    sp.wait_ge(s_added, 1 + 2 * HB * chunk_b(b, k) + (HB if last(b) else 2 * HB))
                    sp.dma_start(x_b[:, :, :], x_d[bass.ds(chunk_b(b, k) + 1, 1)]
                                 .rearrange("o p h t -> p (o h) t")).then_inc(xb_loaded, 16)

            steps(sp, step)
            sp.wait_ge(stored, 16 + 16 * (NB * NK + 1))

        @block.tensor
        def _(pe):
            start(pe, y_done, ff_done)

            def u_products(b, k, directions=(F_, B_)):
                for d in directions:
                    if not (first(b) and k == 0):
                        pe.wait_ge(rotated, rotations(b, k) - (k == 0 or d == F_))
                    if first(b) and k == 0 and d == F_:
                        pe.wait_ge(bt_hi_ready, 1)
                    for c in range(2):
                        for h in range(HB):
                            if d == 0 and c == 0:
                                pe.wait_ge(x_hi_ready, HB * chunk_a(b, k) + h + 1)
                            nc.tensor.matmul(pu[:, d, c, :], bt_hi[:, h, 2 * d + c, :], x_hi[:, k % 2, h, :],
                                             start=(h == 0), stop=False)
                    if first(b) and k == 0:
                        pe.wait_ge(bt_lo_ready, d + 1)
                    for c in range(2):
                        for h in range(HB):
                            nc.tensor.matmul(pu[:, d, c, :], bt_lo[:, h, 2 * d + c, :], x_hi[:, k % 2, h, :],
                                             start=False, stop=False)
                    for c in range(2):
                        for h in range(HB):
                            if d == 0 and c == 0:
                                pe.wait_ge(x_lo_ready, HB * chunk_a(b, k) + h + 1)
                            mm = nc.tensor.matmul(pu[:, d, c, :], bt_hi[:, h, 2 * d + c, :], x_lo[:, k % 2, h, :],
                                                  start=False, stop=(h == HB - 1))
                    mm.then_inc(u_done, 1)

            def y_products(b, k, directions=(F_, B_)):
                n = chunk_b(b, k)
                for d in directions:
                    if d == F_:
                        pe.wait_ge(rotated, rotations(b, k) - (0 if last(b) and k else 2))
                    elif k == 0:
                        pe.wait_ge(rotated, rotations(b, 0))
                    if d == B_ and ahead(b, k) and k > 1:
                        pe.wait_ge(y_read, 2 * HB * (n - 1) + HB)
                    for h in range(HB):
                        if d == B_ and ahead(b, k):
                            acc = pu[:, h // 2, h % 2, :]
                        else:
                            acc = py[:, h, :]
                            if d == F_ and h < 2:
                                pe.wait_ge(w_ready, 1 + TB * n - 1 + h)
                            elif d == F_:
                                pe.wait_ge(t_squared, 1 + TB * n - 3 + h)
                            else:
                                pe.wait_ge(y_read, 2 * HB * n + h + 1)
                        for c in range(2):
                            states = (st_f[:, c, :] if d == F_ else
                                      st_b[:, bass.ds(slot(b - 1, k), 1), c, :].rearrange("p o t -> p (o t)"))
                            mm = nc.tensor.matmul(acc, ct[:, 2 * d + c, P * h:P * h + P], states,
                                                  start=(c == 0), stop=(c == 1))
                        mm.then_inc(y_done, 1)

            def feed_forward(b, k):
                n = chunk_b(b, k)
                pe.wait_ge(y_read, 2 * HB * (n + 1))
                pe.wait_ge(s_added, 1 + 2 * HB * (n + 1))

                def transpose(t):
                    if t >= 2:
                        pe.wait_ge(t_squared, 1 + TB * n + t - 1)
                    for h in range(HB):
                        mm = nc.tensor.transpose(py[:, 2 + t % 2, P * h:P * h + P], s[:, h, P * t:P * t + P],
                                                 ident[:, :])
                    mm.then_inc(t_done, 1)

                def high(t):
                    if t >= 2:
                        pe.wait_ge(w_ready, 1 + TB * n + t - 1)
                    for h in range(HB):
                        nc.tensor.matmul(py[:, t % 2, :], s_hi[:, h, P * t:P * t + P], wc[:, h, :],
                                         start=(h == 0), stop=False)

                def low(t):
                    for h in range(HB):
                        if t == 0:
                            pe.wait_ge(s_lo_ready, HB * n + h + 1)
                        mm = nc.tensor.matmul(py[:, t % 2, :], s_lo[:, h, P * t:P * t + P], wc[:, h, :],
                                              start=False, stop=(h == HB - 1))
                    mm.then_inc(ff_done, 1)

                transpose(0)
                pe.wait_ge(s_hi_ready, HB * (n + 1))
                high(0)
                transpose(1)
                high(1)
                low(0)
                low(1)
                for t in range(2, TB):
                    transpose(t)
                    high(t)
                    low(t)

            def mean_setup():
                pe.wait_ge(abs_sums, 1)
                pe.wait_ge(consts_ready, 1)
                nc.tensor.matmul(py[:, 0, 0:1], ones[:, :], small[:, 40:41], start=True, stop=True)\
                  .then_inc(mean_abs, 1)

            def row_means_setup():
                pe.wait_ge(ternary_ready, 1)
                for h in range(HB):
                    mm = nc.tensor.matmul(py[:, 1, :], ones[:, :], ternary[:, h, :],
                                          start=(h == 0), stop=(h == HB - 1))
                mm.then_inc(row_means, 1)

            def step(b, k):
                if first(b):
                    u_products(b, k)
                elif last(b):
                    y_products(b, k, [F_] if ahead(b, k) else [F_, B_])
                    if ahead(b, k + 1):
                        y_products(b, k + 1, [B_])
                elif k < NK - 1:
                    y_products(b, k)
                    u_products(b, k)
                else:
                    u_products(b, k, [F_])
                    y_products(b, k)
                    u_products(b, k, [B_])
                if not first(b):
                    feed_forward(b, k)
                if first(b) and k == 0:
                    mean_setup()
                if first(b) and k == 2:
                    row_means_setup()
                if first(b) and k == 3:
                    pe.wait_ge(wc_ready, HB)
                    pe.wait_ge(ct_ready, 1)
                    pe.wait_ge(ident_ready, 2)

            steps(pe, step)

        @block.scalar
        def _(act):
            start(act, t_squared, stored)

            act.wait_ge(theta_ready, 1)
            nc.scalar.activation(small[:, 60:62], small[:, 56:58], ACT.Sin)
            nc.scalar.activation(small[:, 58:60], small[:, 62:64], ACT.Sin, scale=-1.0).then_inc(first_sincos, 1)
            act.wait_ge(bt_loaded, 16)
            nc.scalar.activation(bt_hi[:, :, :, :], bt_raw, ACT.Copy).then_inc(bt_hi_ready, 1)

            def tables_setup():
                for d in (F_, B_):
                    act.wait_ge(phase_ready, d + 1)
                    nc.scalar.activation(tab_out[:, d, 1, :], phase[:, d, 0, :], ACT.Sin)
                    nc.scalar.activation(tab_out[:, d, 0, :], phase[:, d, 1, :], ACT.Sin, scale=-1.0)\
                      .then_inc(sincos_ready, 1)
                    if d == F_:
                        act.wait_ge(gain_ready, 1)
                    act.wait_ge(sincos_ready, d + 1)
                    nc.scalar.activation(phase[:, d, 0, :], tab_out[:, d, 1, :], ACT.Identity, scale=gain[:, 2 + d:3 + d])
                    nc.scalar.activation(phase[:, d, 1, :], tab_out[:, d, 1, :], ACT.Identity, scale=gain[:, d:d + 1])\
                      .then_inc(table_products, 1)

            def weights_setup():
                act.wait_ge(wt_loaded, 16)
                nc.scalar.activation(ternary, wt_raw, ACT.Abs, accum_out=small[:, 40:41]).then_inc(abs_sums, 1)
                act.wait_ge(ct_loaded, 32)
                for c in (1, 3):
                    neg = nc.scalar.activation(ct[:, c, :], ct[:, c, :], ACT.Copy, scale=-1.0)
                neg.then_inc(ct_ready, 1)

            def x_high(b, k):
                if not (first(b) and k < 2):
                    act.wait_ge(u_done, 2 * (chunk_a(b, k) - 1))
                act.wait_ge(xa_loaded, 16 * (chunk_a(b, k) + 1))
                for h in range(HB):
                    nc.scalar.activation(x_hi[:, k % 2, h, :], x_a[:, h, :], ACT.Copy).then_inc(x_hi_ready, 1)

            def final(b, k):
                n = chunk_b(b, k)
                act.wait_ge(shift_ready, n + 1)
                halves = 2 if last(b) and k == NK - 1 else 1
                rows = TB // halves
                for i in range(halves):
                    ts = range(rows * i, rows * (i + 1))
                    for t in ts:
                        fin = nc.scalar.activation(w[:, t, :], w[:, t, :], ACT.Identity,
                                                   bias=shift[:, t:t + 1], scale=rstd[:, t:t + 1])
                    fin.then_inc(final_ready, 1)
                    act.wait_ge(final_ready, n + 1 + i)
                    act.dma_start(out_d[bass.ds(n, 1), P * ts[0]:P * (ts[-1] + 1), :]
                                  .rearrange("o (t p) h -> p (o t) h", p=P), w[:, ts[0]:ts[-1] + 1, :])\
                       .then_inc(stored, 16)

            x_high(0, 0)

            def step(b, k):
                if first(b) and k == 0:
                    tables_setup()
                if not first(b):
                    n = chunk_b(b, k)

                    def s_high(h):
                        act.wait_ge(s_added, 1 + 2 * HB * n + HB + h + 1)
                        nc.scalar.activation(s_hi[:, h, :], s[:, h, :], ACT.Copy).then_inc(s_hi_ready, 1)

                    def gelu(n, j):
                        act.wait_ge(y_read, 2 * HB * n + j + 1)
                        nc.scalar.activation(y[:, j, :], y[:, j, :], ACT.Gelu).then_inc(gelu_ready, 1)

                    here, early = outputs(b, k)
                    for j in here:
                        if k and j == (6 if last(b) else 0 if k == NK - 1 else 2):
                            final(b, k - 1)
                        gelu(n, j)
                        if j >= HB + 2:
                            s_high(j - HB - 2)
                    s_high(HB - 2)
                    s_high(HB - 1)
                if not last(b):
                    x_high(*following(b, k))
                if first(b) and k == 0:
                    weights_setup()
                if first(b) and k == NK - 1:
                    act.wait_ge(row_means, 1)
                    nc.scalar.activation(means, py[:, 1, :], ACT.Copy).then_inc(means_copied, 1)
                if not first(b):
                    for t in range(TB):
                        act.wait_ge(t_done, TB * n + t + 1)
                        act.wait_ge(w_ready, 1 + TB * n + max(t - 1, 0))
                        bank = py[:, 2 + t % 2, :]
                        nc.scalar.activation(s_t[:, t % 2, :], bank, ACT.Copy,
                                             accum_out=sums[:, 0, t:t + 1]).then_inc(t_copied, 1)
                        act.wait_ge(t_copied, TB * n + t + 1)
                        nc.scalar.activation(bank, bank, ACT.Square,
                                             accum_out=sums[:, 1, t:t + 1]).then_inc(t_squared, 1)
                    for j in early:
                        gelu(n + 1, j)
                    if k == NK - 1:
                        final(b, k)

            steps(act, step)

        @block.gpsimd
        def _(pool):
            start(pool, s_added)

            count = [0]

            def link(ins):
                count[0] += 1
                ins.then_inc(pool_step, 1)
                pool.wait_ge(pool_step, count[0])

            nc.gpsimd.memset(minus_half[:, :], -0.5)
            link(nc.gpsimd.memset(small[:, 44:48], float(np.e)))
            pool.wait_ge(par_loaded, 16)
            nc.gpsimd.tensor_tensor(small[:, 8:12], small[:, 44:48], small[:, 0:4], ALU.pow).then_inc(exps_ready, 1)
            nc.gpsimd.memset(ones[:, :], 1.0 / H).then_inc(consts_ready, 1)
            nc.gpsimd.memset(ident[:, :], 0.0).then_inc(ident_ready, 1)
            pool.wait_ge(ident_ready, 1)
            nc.gpsimd.affine_select(out=ident[:, :], in_=ident[:, :], compare_op=ALU.not_equal, fill=1.0,
                                    base=0, pattern=[[-1, P]], channel_multiplier=1).then_inc(ident_ready, 1)

            def tt(out, a, b_, op):
                link(nc.gpsimd.tensor_tensor(out, a, b_, op))

            def ts(out, a, s1, s2, op1, op2=None):
                link(nc.gpsimd.tensor_scalar(out, a, s1, s2, op1, op2) if op2 else
                     nc.gpsimd.tensor_scalar(out, a, s1, s2, op1))

            def modulus_setup():
                pool.wait_ge(exps_ready, 1)
                tt(lam_re, small[:, 8:10], small[:, 8:10], ALU.mult)
                tt(is_small, small[:, 4:6], small[:, 4:6], ALU.mult)
                tt(is_small, is_small, lam_re, ALU.add)
                ts(is_small, is_small, LAM_MIN ** 2, None, ALU.is_lt)
                ts(keep, is_small, -1.0, 1.0, ALU.mult, ALU.add)
                ts(is_small, is_small, LAM_MIN, None, ALU.mult)
                tt(lam_re, small[:, 8:10], keep, ALU.mult)
                tt(lam_re, is_small, lam_re, ALU.subtract)
                tt(lam_im, small[:, 4:6], keep, ALU.mult)
                tt(modulus, lam_re, lam_re, ALU.mult)
                tt(temp, lam_im, lam_im, ALU.mult)
                nc.gpsimd.tensor_tensor(modulus, modulus, temp, ALU.add).then_inc(modulus_ready, 1)

            def gain_setup():
                pool.wait_ge(first_sincos, 1)
                pool.wait_ge(decay_ready, 1)
                tt(lr, small[:, 58:60], rho[:, :], ALU.mult)
                tt(li, small[:, 60:62], rho[:, :], ALU.mult)
                ts(lr, lr, -1.0, None, ALU.add)
                tt(gain[:, 0:2], lr, lam_re, ALU.mult)
                tt(temp, li, lam_im, ALU.mult)
                tt(gain[:, 0:2], gain[:, 0:2], temp, ALU.add)
                tt(gain[:, 2:4], li, lam_re, ALU.mult)
                tt(temp, lr, lam_im, ALU.mult)
                tt(gain[:, 2:4], gain[:, 2:4], temp, ALU.subtract)
                pool.wait_ge(inverse_ready, 1)
                nc.gpsimd.tensor_tensor(gain[:, 0:2], gain[:, 0:2], modulus, ALU.mult)
                nc.gpsimd.tensor_tensor(gain[:, 2:4], gain[:, 2:4], modulus, ALU.mult).then_inc(gain_ready, 1)

            modulus_setup()
            pool.wait_ge(exponent_ready, 1)
            nc.gpsimd.tensor_tensor(rho[:, :], small[:, 44:46], small[:, 12:14], ALU.pow).then_inc(decay_ready, 1)

            def weights_low(d):
                pool.wait_ge(bt_hi_ready, 1)
                c = slice(2 * d, 2 * d + 2)
                nc.gpsimd.tensor_tensor(bt_lo[:, :, c, :], bt_raw[:, :, c, :], bt_hi[:, :, c, :].bitcast(f32),
                                        ALU.subtract).then_inc(bt_lo_ready, 1)

            def ternary_setup():
                pool.wait_ge(thresholds, 1)
                link(nc.gpsimd.tensor_scalar(ternary, wt_raw, small[:, 41:42], None, ALU.is_gt))
                link(nc.gpsimd.tensor_scalar(wt_raw, wt_raw, small[:, 42:43], None, ALU.is_lt))
                nc.gpsimd.tensor_tensor(ternary, ternary, wt_raw, ALU.subtract).then_inc(ternary_ready, 1)

            def centre_setup():
                pool.wait_ge(means_copied, 1)
                for h in range(HB):
                    nc.gpsimd.tensor_tensor(wc[:, h, :], ternary[:, h, :], means, ALU.subtract)\
                      .then_inc(wc_ready, 1)

            def x_low(b, k):
                for h in range(HB):
                    pool.wait_ge(x_hi_ready, HB * chunk_a(b, k) + h + 1)
                    nc.gpsimd.tensor_tensor(x_lo[:, k % 2, h, :], x_a[:, h, :], x_hi[:, k % 2, h, :].bitcast(f32),
                                            ALU.subtract)\
                      .then_inc(x_lo_ready, 1)

            def norm_factors(b, k):
                n = chunk_b(b, k)
                pool.wait_ge(var_ready, n + 1)
                nc.gpsimd.tensor_tensor(rstd[:, :], var_e[:, :], minus_half[:, :], ALU.pow).then_inc(rstd_ready, 1)
                pool.wait_ge(rstd_ready, n + 1)
                nc.gpsimd.tensor_tensor(shift[:, :], neg_mean[:, :], rstd[:, :], ALU.mult).then_inc(shift_ready, 1)

            weights_low(F_)
            gain_setup()
            x_low(0, 0)
            weights_low(B_)

            def step(b, k):
                if not first(b):
                    here, early = outputs(b, k)
                    if k and not last(b):
                        norm_factors(b, k - 1)
                    n = chunk_b(b, k)

                    def s_low(h):
                        pool.wait_ge(s_hi_ready, HB * n + h + 1)
                        nc.gpsimd.tensor_tensor(s_lo[:, h, :], s[:, h, :], s_hi[:, h, :].bitcast(f32),
                                                ALU.subtract).then_inc(s_lo_ready, 1)

                    def add(n, j):
                        h = j % HB
                        if j == 0:
                            pool.wait_ge(xb_loaded, 16 * (n + 1))
                            pool.wait_ge(ff_done, 1 + TB * n)
                        pool.wait_ge(gelu_ready, 2 * HB * n + j + 1)
                        if j >= HB:
                            pool.wait_ge(s_added, 1 + 2 * HB * n + h + 1)
                        nc.gpsimd.tensor_tensor(s[:, h, :], (x_b if j < HB else s)[:, h, :], y[:, j, :],
                                                ALU.add).then_inc(s_added, 1)

                    for j in here:
                        add(n, j)
                    for h in range(HB):
                        s_low(h)
                if first(b) and k == NK - 1:
                    centre_setup()
                if not last(b):
                    x_low(*following(b, k))
                if first(b) and k == 1:
                    ternary_setup()
                if not first(b):
                    for j in early:
                        add(n + 1, j)
                    if k == NK - 1 or last(b):
                        norm_factors(b, k)

            steps(pool, step)

        @block.vector
        def _(dve):
            start(dve, w_ready)

            count = [0]

            def link(ins):
                count[0] += 1
                ins.then_inc(setup_step, 1)
                dve.wait_ge(setup_step, count[0])

            V = nc.vector

            def tables_setup():
                jv = z
                link(V.memset(st_f[:, 0, :], 1.0))
                link(V.tensor_tensor_scan(jv[:, 0, :], st_f[:, 0, :], st_f[:, 0, :], 0.0, ALU.mult, ALU.add))
                link(V.tensor_copy(jv[:, 1, ::-1], jv[:, 0, :]))
                dve.wait_ge(exps_ready, 1)
                delta, theta = small[:, 10:12], small[:, 14:16]
                link(V.scalar_tensor_tensor(out=small[:, 12:14], in0=small[:, 8:10], scalar=-1.0, in1=delta,
                                            op0=ALU.mult, op1=ALU.mult))
                V.tensor_tensor(theta, small[:, 4:6], delta, ALU.mult).then_inc(exponent_ready, 1)
                dve.wait_ge(exponent_ready, 1)
                turns, th_lo = small[:, 16:18], small[:, 20:22]
                link(V.tensor_scalar(turns, theta, 1 / TWO_PI, MAGIC, ALU.mult, ALU.add))
                link(V.tensor_scalar(turns, turns, MAGIC, None, ALU.subtract))
                for part in (PI_1, PI_2, PI_3):
                    link(V.scalar_tensor_tensor(out=theta, in0=turns, scalar=-part, in1=theta,
                                                op0=ALU.mult, op1=ALU.add))
                first_sin, first_cos = small[:, 56:58], small[:, 62:64]
                link(V.tensor_scalar(first_sin, theta, PI_DOWN, -PI_DOWN, ALU.min, ALU.max))
                link(V.scalar_tensor_tensor(out=first_cos, in0=first_sin, scalar=-1.0, in1=first_sin,
                                            op0=ALU.mult, op1=ALU.max))
                V.tensor_scalar(first_cos, first_cos, float(np.pi / 2), None, ALU.subtract).then_inc(theta_ready, 1)
                link(V.tensor_copy(th_hi[:, :], theta))
                link(V.tensor_tensor(th_lo, theta, th_hi[:, :].bitcast(f32), ALU.subtract))
                for d in (F_, B_):
                    ph, q = phase[:, d, 0, :], phase[:, d, 1, :]
                    link(V.tensor_scalar(ph, jv[:, d, :], th_hi[:, d:d + 1].bitcast(f32), None, ALU.mult))
                    link(V.tensor_scalar(q, jv[:, d, :], theta[:, d:d + 1], 1 / TWO_PI, ALU.mult, ALU.mult))
                    link(V.tensor_scalar(q, q, MAGIC, MAGIC, ALU.add, ALU.subtract))
                    link(V.scalar_tensor_tensor(out=ph, in0=q, scalar=-PI_1, in1=ph, op0=ALU.mult, op1=ALU.add))
                    link(V.scalar_tensor_tensor(out=ph, in0=q, scalar=-PI_2, in1=ph, op0=ALU.mult, op1=ALU.add))
                    link(V.scalar_tensor_tensor(out=ph, in0=jv[:, d, :], scalar=th_lo[:, d:d + 1], in1=ph,
                                                op0=ALU.mult, op1=ALU.add))
                    link(V.tensor_scalar(ph, ph, PI_DOWN, -PI_DOWN, ALU.min, ALU.max))
                    link(V.scalar_tensor_tensor(out=q, in0=ph, scalar=-1.0, in1=ph, op0=ALU.mult, op1=ALU.max))
                    V.tensor_scalar(q, q, float(np.pi / 2), None, ALU.subtract).then_inc(phase_ready, 1)
                    if d == F_:
                        dve.wait_ge(modulus_ready, 1)
                        V.reciprocal(modulus, modulus).then_inc(inverse_ready, 1)

            def tab_in_setup(d):
                dve.wait_ge(table_products, d + 1)
                if d == F_:
                    dve.wait_ge(gain_ready, 1)
                cos = tab_out[:, d, 0, :]
                V.scalar_tensor_tensor(out=tab_in[:, d, 0, :], in0=cos, scalar=gain[:, d:d + 1],
                                       in1=phase[:, d, 0, :], op0=ALU.mult, op1=ALU.add)
                link(V.scalar_tensor_tensor(out=tab_in[:, d, 1, :], in0=cos, scalar=gain[:, 2 + d:3 + d],
                                            in1=phase[:, d, 1, :], op0=ALU.mult, op1=ALU.subtract))

            def ternary_setup():
                dve.wait_ge(mean_abs, 1)
                link(V.tensor_scalar(scale[:, :], py[:, 0, 0:1], 1.0 / H, EPS, ALU.mult, ALU.max))
                link(V.tensor_scalar(small[:, 41:42], scale[:, :], 0.5, None, ALU.mult))
                V.tensor_scalar(small[:, 42:43], scale[:, :], -0.5, None, ALU.mult).then_inc(thresholds, 1)

            def wide(table):
                return table.to_broadcast([P, 2, T])

            def rotate_in(b, k, d, done):
                n = 2 * chunk_a(b, k) + d
                dve.wait_ge(rotated, done)
                dve.wait_ge(u_done, n + 1)
                V.tensor_tensor(prod[:, 0, :, :], pu[:, d, :, :], wide(tab_in[:, d, 0:1, :]), ALU.mult)
                V.tensor_tensor(pu[:, d, :, :], pu[:, d, :, :], wide(tab_in[:, d, 1:2, :]), ALU.mult)\
                 .then_inc(in_products, 1)
                dve.wait_ge(in_products, n + 1)
                if d == F_:
                    sl = bass.ds(slot(b, NK - 1 - k), 1)
                    re, im = v_f[:, sl, 0, :], v_f[:, sl, 1, :]
                    re, im = (v.rearrange("p o t -> p (o t)") for v in (re, im))
                else:
                    re, im = v_b[:, 0, :], v_b[:, 1, :]
                V.tensor_tensor(re, prod[:, 0, 0, :], pu[:, d, 1, :], ALU.subtract)
                V.tensor_tensor(im, prod[:, 0, 1, :], pu[:, d, 0, :], ALU.add).then_inc(rotated, 1)

            def rotate_out(n, d, re, im, z_ready, products):
                dve.wait_ge(z_ready, n + 1)
                V.tensor_tensor(prod[:, 0, :, :], z[:, :, :], wide(tab_out[:, d, 0:1, :]), ALU.mult)
                V.tensor_tensor(prod[:, 1, :, :], z[:, :, :], wide(tab_out[:, d, 1:2, :]), ALU.mult)\
                 .then_inc(products, 1)
                dve.wait_ge(products, n + 1)
                V.tensor_tensor(re, prod[:, 0, 0, :], prod[:, 1, 1, :], ALU.subtract)
                V.tensor_tensor(im, prod[:, 0, 1, :], prod[:, 1, 0, :], ALU.add).then_inc(rotated, 1)

            def scan_b(b, k, c, done):
                dve.wait_ge(rotated, done)
                if k == 0:
                    init = 0.0
                else:
                    init = st_b[:, bass.ds(slot(b, NK - k), 1), c, 0:1].rearrange("p o t -> p (o t)")
                op = V.tensor_tensor_scan(z[:, c, ::-1], rho[:, B_:B_ + 1].to_broadcast([P, T]), v_b[:, c, ::-1],
                                          init, ALU.mult, ALU.add)
                if c:
                    op.then_inc(zb_ready, 1)

            def out_b(b, k):
                sl = bass.ds(slot(b, NK - 1 - k), 1)
                re, im = (st_b[:, sl, c, :].rearrange("p o t -> p (o t)") for c in range(2))
                if not first(b):
                    dve.wait_ge(y_done, 1 + 2 * HB * (chunk_b(b, k) + 1))
                rotate_out(chunk_a(b, k), B_, re, im, zb_ready, outb_products)

            def scan_f(b, k, c, done):
                dve.wait_ge(rotated, done)
                if k == 0:
                    init = 0.0
                else:
                    init = st_f[:, c, T - 1:T]
                sl = bass.ds(slot(b - 1, k), 1)
                op = V.tensor_tensor_scan(z[:, c, :], rho[:, F_:F_ + 1].to_broadcast([P, T]),
                                          v_f[:, sl, c, :].rearrange("p o t -> p (o t)"), init, ALU.mult, ALU.add)
                if c:
                    op.then_inc(zf_ready, 1)

            def out_f(b, k):
                n = chunk_b(b, k)
                rotate_out(n, F_, st_f[:, 0, :], st_f[:, 1, :], zf_ready, outf_products)

            def read_y(b, k, j):
                n = chunk_b(b, k)
                half, h = divmod(j, HB)
                d = 1 - half if ahead(b, k) else half
                bank = pu[:, h // 2, h % 2, :] if ahead(b, k) and d == B_ else py[:, h, :]
                if j == 0:
                    dve.wait_ge(xb_loaded, 16 * (n + 1))
                if k:
                    dve.wait_ge(s_added, 1 + 2 * HB * n - (2 * HB - 1 - j))
                elif j == 0:
                    dve.wait_ge(s_added, 1 + 2 * HB * n)
                dve.wait_ge(y_done, 1 + 2 * HB * n + j + 1)
                V.scalar_tensor_tensor(out=y[:, j, :], in0=x_b[:, h, :], scalar=d_sb[:, d, h:h + 1],
                                       in1=bank, op0=ALU.mult, op1=ALU.add).then_inc(y_read, 1)

            def norm(b, k, between=()):
                n = chunk_b(b, k)
                between = list(between)
                dve.wait_ge(stored, 16 + 16 * n)
                for t in range(TB):
                    dve.wait_ge(t_copied, TB * n + t + 1)
                    dve.wait_ge(ff_done, 1 + TB * n + t + 1)
                    V.scalar_tensor_tensor(out=w[:, t, :], in0=py[:, t % 2, :], scalar=scale[:, 0:1],
                                           in1=s_t[:, t % 2, :], op0=ALU.mult, op1=ALU.add).then_inc(w_ready, 1)
                    if t == TB - 1:
                        while between:
                            between.pop(0)()
                    dve.wait_ge(w_ready, 1 + TB * n + t + 1)
                    V.bn_stats(stats[:, t, :], w[:, t, :]).then_inc(stats_ready, 1)
                    if between and t < 2:
                        between.pop(0)()
                dve.wait_ge(stats_ready, TB * (n + 1))
                dve.wait_ge(t_squared, 1 + TB * (n + 1))
                V.tensor_tensor(mean_gap[:, :], stats[:, :, 1], stats[:, :, 4], ALU.subtract)
                V.tensor_tensor(mean_sum[:, :], stats[:, :, 1], stats[:, :, 4], ALU.add).then_inc(halves_read, 1)
                V.tensor_tensor(sq_sum[:, :], stats[:, :, 2], stats[:, :, 5], ALU.add)
                V.scalar_tensor_tensor(out=mean_sq[:, :], in0=sums[:, 0, :], scalar=-1 / H, in1=sums[:, 0, :],
                                       op0=ALU.mult, op1=ALU.mult)
                dve.wait_ge(halves_read, n + 1)
                V.scalar_tensor_tensor(out=gap_sq[:, :], in0=mean_gap[:, :], scalar=H / 4, in1=mean_gap[:, :],
                                       op0=ALU.mult, op1=ALU.mult).then_inc(gap_squared, 1)
                V.tensor_scalar(neg_mean[:, :], mean_sum[:, :], -0.5, None, ALU.mult)
                dve.wait_ge(gap_squared, n + 1)
                V.tensor_tensor(gap_sq[:, :], gap_sq[:, :], sq_sum[:, :], ALU.add)
                V.tensor_tensor(mean_sq[:, :], mean_sq[:, :], sums[:, 1, :], ALU.add).then_inc(sq_ready, 1)
                dve.wait_ge(sq_ready, n + 1)
                V.scalar_tensor_tensor(out=var_e[:, :], in0=mean_sq[:, :], scalar=EPS, in1=gap_sq[:, :],
                                       op0=ALU.mult, op1=ALU.add).then_inc(eps_var, 1)
                dve.wait_ge(eps_var, n + 1)
                V.tensor_scalar(var_e[:, :], var_e[:, :], 1 / H, EPS * EPS, ALU.mult, ALU.add).then_inc(var_ready, 1)

            def step(b, k):
                fill = []
                done = rotations(b, k)

                def backward(b, k, done):
                    return [lambda: scan_b(b, k, 0, done), lambda: scan_b(b, k, 1, done), lambda: out_b(b, k)]

                if k and not last(b):
                    fill = backward(b, k - 1, done)
                if not first(b):
                    if not last(b) and k == NK - 1:
                        while fill:
                            fill.pop(0)()
                        fill = [lambda: rotate_in(b, k, F_, out_f_done(b, k) - 2)]
                    here, early = outputs(b, k)
                    for j in here:
                        read_y(b, k, j)
                        if fill:
                            fill.pop(0)()
                while fill:
                    fill.pop(0)()
                def next_forward():
                    nb, nk = (b, k + 1) if k < NK - 1 else (b + 1, 0)
                    before = out_f_done(b, k) - 1
                    scan_f(nb, nk, 0, before)
                    scan_f(nb, nk, 1, before)
                    out_f(nb, nk)

                if not first(b) and k < NK - 1:
                    next_forward()
                if not last(b):
                    if k < NK - 1:
                        done = done + (k > 0) if first(b) else out_f_done(b, k)
                        rotate_in(b, k, F_, done)
                        if first(b) and k == 0:
                            tab_in_setup(B_)
                        rotate_in(b, k, B_, done + 1)
                        if first(b) and k == 0:
                            ternary_setup()
                    else:
                        if first(b):
                            rotate_in(b, k, F_, out_f_done(b, k) - 2)
                        next_forward()
                        rotate_in(b, k, B_, out_f_done(b, k))
                        fill = backward(b, k, out_f_done(b, k) + 1)
                        if first(b):
                            for op in fill:
                                op()
                if not first(b):
                    for j in early:
                        read_y(b, k + 1, j)
                    norm(b, k, fill)

            tables_setup()
            tab_in_setup(F_)
            steps(dve, step)


def kernel(**inputs):
    import numpy as _np
    import concourse.bacc as _bacc
    from concourse import mybir as _mybir
    from concourse.bass_utils import run_bass_kernel_spmd as _run

    a = {n.removeprefix("L0_").removeprefix("attn_"): _np.asarray(v) for n, v in inputs.items()}
    arrays = {
        "x": a["x"].reshape(NB * NK, T, HB, P).transpose(0, 3, 2, 1),
        "bt": _np.stack([a[f"{d}_B_{c}"].T.reshape(HB, P, P) for d in ("fwd", "bwd")
                         for c in ("real", "imag")], 2).transpose(1, 0, 2, 3),
        "ct": _np.stack([a[f"{d}_C_{c}"].T for d in ("fwd", "bwd") for c in ("real", "imag")], 1),
        "wt": a["ffn_weight"].T.reshape(HB, P, H).transpose(1, 0, 2),
        "d": _np.stack([a["fwd_D"].reshape(HB, P).T, a["bwd_D"].reshape(HB, P).T], 1),
        "par": _np.stack([a["fwd_log_real"], a["bwd_log_real"], a["fwd_log_Delta"], a["bwd_log_Delta"],
                          a["fwd_imag"], a["bwd_imag"]], 1),
    }
    arrays = {n: _np.ascontiguousarray(v) for n, v in arrays.items()}
    nc = _bacc.Bacc("TRN2", target_bir_lowering=False, num_devices=1)
    args = [nc.dram_tensor(f"{n}_dram", v.shape, _mybir.dt.from_np(v.dtype), kind="ExternalInput").ap()
            for n, v in arrays.items()]
    out = nc.dram_tensor("out_dram", (NB * NK, T, H), _mybir.dt.float32, kind="ExternalOutput").ap()
    build(nc, *args, out)
    r = _run(nc, [{f"{n}_dram": v for n, v in arrays.items()}], core_ids=[0])
    return r.results[0]["out_dram"].reshape(NB, L, H)
```

```python
import concourse.bass as bass
from concourse import mybir
from contextlib import ExitStack
import numpy as np

P = 128
NB, L, H = 4, 2048, 512
T = 512
NK = L // T
HB = H // P
TB = T // P
EPS = 1e-5
LAM_MIN = 1e-6
MAGIC = 12582912.0
TWO_PI = 2 * np.pi
PI_1 = float(np.float32(6.28125))
PI_2 = float(np.float32(TWO_PI - PI_1))
PI_3 = float(np.float32(TWO_PI - PI_1 - PI_2))
PI_DOWN = float(np.nextafter(np.float32(np.pi), np.float32(0)))
F_, B_ = 0, 1


def build(nc, x_d, bt_d, ct_d, wt_d, d_d, par_d, out_d):
    f32, f32r = mybir.dt.float32, mybir.dt.float32r
    ALU = mybir.AluOpType
    ACT = mybir.ActivationFunctionType

    ctx = ExitStack()
    with ctx:
        def sb(name, shape, dt=f32):
            return ctx.enter_context(nc.sbuf_tensor(name, [P] + shape, dt))

        def sem(name):
            return ctx.enter_context(nc.semaphore(name))

        x_a = sb("x_a", [HB, T])
        x_hi = sb("x_hi", [2, HB, T], f32r)
        x_lo = sb("x_lo", [2, HB, T], f32r)
        x_b = sb("x_b", [HB, T])
        bt_hi = sb("bt_hi", [HB, 4, P], f32r)
        bt_lo = sb("bt_lo", [HB, 4, P], f32r)
        ct = sb("ct", [4, H])
        wc = sb("wc", [HB, H], f32r)
        d_sb = sb("d_sb", [2, HB])
        tab_in = sb("tab_in", [2, 2, T])
        tab_out = sb("tab_out", [2, 2, T])
        v_f = sb("v_f", [NK, 2, T])
        st_b = sb("st_b", [NK, 2, T])
        z = sb("z", [2, T])
        st_f = sb("st_f", [2, T])
        prod = sb("prod", [2, 2, T])
        y = sb("y", [2 * HB, T])
        s = sb("s", [HB, T])
        s_hi = sb("s_hi", [HB, T], f32r)
        s_lo = sb("s_lo", [HB, T], f32r)
        s_t = sb("s_t", [2, H])
        w = sb("w", [TB, H])
        sums = sb("sums", [2, TB])
        stats = sb("stats", [TB, 6])
        mean_sum = sb("mean_sum", [TB])
        mean_gap = sb("mean_gap", [TB])
        sq_sum = sb("sq_sum", [TB])
        var_w = sb("var_w", [TB])
        var_s = sb("var_s", [TB])
        var_e = sb("var_e", [TB])
        neg_mean = sb("neg_mean", [TB])
        rstd = sb("rstd", [TB])
        shift = sb("shift", [TB])
        ident = sb("ident", [P])
        over_h = sb("over_h", [P])
        minus_half = sb("minus_half", [TB])
        rho = sb("rho", [2])
        scale = sb("scale", [1])

        pu = ctx.enter_context(nc.psum_tensor("pu", [P, 2, 2, T], f32))
        py = ctx.enter_context(nc.psum_tensor("py", [P, 4, T], f32))

        bt_loaded, out_weights_loaded, wt_loaded, par_loaded = map(sem, (
            "bt_loaded", "out_weights_loaded", "wt_loaded", "par_loaded"))
        over_h_ready, ident_ready = sem("over_h_ready"), sem("ident_ready")
        bt_hi_ready, bt_lo_ready = sem("bt_hi_ready"), sem("bt_lo_ready")
        ct_ready = sem("ct_ready")
        exps_ready, decay_ready, theta_ready = sem("exps_ready"), sem("decay_ready"), sem("theta_ready")
        first_sincos, modulus_ready, inverse_ready = map(sem, ("first_sincos", "modulus_ready", "inverse_ready"))
        gain_ready, table_products = sem("gain_ready"), sem("table_products")
        exponent_ready = sem("exponent_ready")
        phase_ready, sincos_ready = sem("phase_ready"), sem("sincos_ready")
        abs_sums, mean_abs, thresholds = sem("abs_sums"), sem("mean_abs"), sem("thresholds")
        ternary_ready, row_means, wc_ready = sem("ternary_ready"), sem("row_means"), sem("wc_ready")
        means_copied = sem("means_copied")
        setup_step, pool_step = sem("setup_step"), sem("pool_step")
        xa_loaded = sem("xa_loaded")
        x_hi_ready, x_lo_ready = sem("x_hi_ready"), sem("x_lo_ready")
        u_done = sem("u_done")
        in_products = sem("in_products")
        zb_ready, outb_products = sem("zb_ready"), sem("outb_products")
        rotated = sem("rotated")
        xb_loaded = sem("xb_loaded")
        zf_ready, outf_products = sem("zf_ready"), sem("outf_products")
        y_done, y_read = sem("y_done"), sem("y_read")
        gelu_ready, s_added = sem("gelu_ready"), sem("s_added")
        s_hi_ready, s_lo_ready = sem("s_hi_ready"), sem("s_lo_ready")
        t_done, t_copied, t_squared = sem("t_done"), sem("t_copied"), sem("t_squared")
        ff_done, w_ready = sem("ff_done"), sem("w_ready")
        stats_ready = sem("stats_ready")
        halves_read, gap_squared, vars_ready = sem("halves_read"), sem("gap_squared"), sem("vars_ready")
        eps_added, var_ready = sem("eps_added"), sem("var_ready")
        rstd_ready, shift_ready = sem("rstd_ready"), sem("shift_ready")
        final_ready, stored = sem("final_ready"), sem("stored")

        def first(b):
            return isinstance(b, int) and b == 0

        def last(b):
            return isinstance(b, int) and b == NB

        def chunk_a(b, k):
            return NK * b + k

        def chunk_b(b, k):
            return NK * (b - 1) + k

        def ahead(b, k):
            return last(b) and 0 < k < NK

        def outputs(b, k):
            here = range(HB if ahead(b, k) else 0, 2 * HB)
            return here, range(HB if ahead(b, k + 1) else 0)

        def u_banks(b, k):
            if first(b) and k % 2 == 0:
                return py[:, :, :].rearrange("p (d c) t -> p d c t", d=2)
            return pu[:, :, :, :]

        def following(b, k):
            return (b, k + 1) if k < NK - 1 else (b + 1, 0)

        def slot(b, pos):
            return pos + (b % 2) * (NK - 1 - 2 * pos)

        def rotations(b, k):
            if first(b):
                return 3 * k - 1 if k else 0
            begun = 3 * NK + 1 + 4 * NK * (b - 1)
            if last(b):
                return begun + k
            return begun + (4 * k - 1 if k else 0)

        def forward_ready(b, k):
            if last(b) and k:
                return rotations(b, k)
            return rotations(b, k) - (1 if k == 1 else 2)

        def start(eng, *sems):
            for x in sems:
                eng.sem_inc(x, 16 if x is stored else 1)

        def steps(eng, step):
            for k in range(NK):
                step(0, k)
            with eng.Fori(1, NB) as b:
                for k in range(NK):
                    step(b, k)
            for k in range(NK):
                step(NB, k)

        bt_raw = s[:, :, :].rearrange("p h (c q) -> p h c q", c=4)
        wt_raw = y[:, 0:HB, :]
        ternary = w[:, :, :]
        phase = y[:, HB:2 * HB, :].rearrange("p (d c) t -> p d c t", d=2)
        means = s_t[:, 0, :]
        th_hi = sb("th_hi", [2], f32r)

        par = sb("par", [6])
        log_re_delta, lambda_im = par[:, 0:4], par[:, 4:6]
        exps = sb("exps", [4])
        minus_re, delta = exps[:, 0:2], exps[:, 2:4]
        e_const = sb("e_const", [4])
        pairs = sb("pairs", [13, 2])
        (exponent, theta, turns, th_lo, lam_re, lam_im, is_small, keep, modulus, temp, lr, li,
         first_cos) = (pairs[:, i, :] for i in range(13))
        first_phase = sb("first_phase", [2, 2])
        first_sin = sb("first_sin", [2])
        gain = sb("gain", [4])
        abs_sum, half_scale = sb("abs_sum", [1]), sb("half_scale", [1])
        minus_half_scale = sb("minus_half_scale", [1])

        block = ctx.enter_context(nc.Block())

        @block.sync
        def _(sp):
            sp.dma_start(par[:, :], par_d).then_inc(par_loaded, 16)
            sp.dma_start(bt_raw, bt_d).then_inc(bt_loaded, 16)

            def load_a(b, k):
                if not (first(b) and k == 0):
                    sp.wait_ge(x_lo_ready, HB * chunk_a(b, k))
                sp.dma_start(x_a[:, :, :], x_d[bass.ds((NK * b) % (NK * NB) + (NK - 1 - k), 1)]
                             .rearrange("o p h t -> p (o h) t")).then_inc(xa_loaded, 16)

            load_a(0, 0)

            def step(b, k):
                if first(b) and k == 0:
                    sp.dma_start(wt_raw, wt_d).then_inc(wt_loaded, 16)
                    sp.dma_start(ct[:, :, :], ct_d).then_inc(out_weights_loaded, 16)
                    sp.dma_start(d_sb[:, :, :], d_d).then_inc(out_weights_loaded, 16)
                if not last(b):
                    load_a(*following(b, k))
                if first(b) and k == NK - 1:
                    sp.dma_start(x_b[:, :, :], x_d[0]).then_inc(xb_loaded, 16)
                if not first(b) and not (last(b) and k == NK - 1):
                    if last(b):
                        sp.wait_ge(y_read, 2 * HB * (chunk_b(b, k) + 1))
                    sp.wait_ge(s_added, 1 + 2 * HB * chunk_b(b, k) + (HB if last(b) else 2 * HB))
                    sp.dma_start(x_b[:, :, :], x_d[bass.ds(chunk_b(b, k) + 1, 1)]
                                 .rearrange("o p h t -> p (o h) t")).then_inc(xb_loaded, 16)

            steps(sp, step)
            sp.wait_ge(stored, 16 + 16 * (NB * NK + 1))

        @block.tensor
        def _(pe):
            start(pe, y_done, ff_done)

            def u_products(b, k, directions=(F_, B_)):
                u = u_banks(b, k)
                for d in directions:
                    if first(b) and k >= 2:
                        pe.wait_ge(rotated, rotations(b, k - 1) + (-1 if d == F_ else 1))
                    elif not first(b):
                        pe.wait_ge(rotated, rotations(b, k) + (-1 if d == F_ else k > 0))
                    if first(b) and k == 1 and d == B_:
                        pe.wait_ge(thresholds, 1)
                    if first(b) and k == 0 and d == F_:
                        pe.wait_ge(bt_hi_ready, 1)
                    for c in range(2):
                        for h in range(HB):
                            if d == 0 and c == 0:
                                pe.wait_ge(x_hi_ready, HB * chunk_a(b, k) + h + 1)
                            nc.tensor.matmul(u[:, d, c, :], bt_hi[:, h, 2 * d + c, :], x_hi[:, k % 2, h, :],
                                             start=(h == 0), stop=False)
                    if first(b) and k == 0:
                        pe.wait_ge(bt_lo_ready, d + 1)
                    for c in range(2):
                        for h in range(HB):
                            nc.tensor.matmul(u[:, d, c, :], bt_lo[:, h, 2 * d + c, :], x_hi[:, k % 2, h, :],
                                             start=False, stop=False)
                    for c in range(2):
                        for h in range(HB):
                            if d == 0 and c == 0:
                                pe.wait_ge(x_lo_ready, HB * chunk_a(b, k) + h + 1)
                            mm = nc.tensor.matmul(u[:, d, c, :], bt_hi[:, h, 2 * d + c, :], x_lo[:, k % 2, h, :],
                                                  start=False, stop=(h == HB - 1))
                    mm.then_inc(u_done, 1)

            def y_products(b, k, directions=(F_, B_)):
                n = chunk_b(b, k)
                for d in directions:
                    if d == F_:
                        pe.wait_ge(rotated, forward_ready(b, k))
                    elif k == 0:
                        pe.wait_ge(rotated, rotations(b, 0))
                    if d == B_ and ahead(b, k) and k > 1:
                        pe.wait_ge(y_read, 2 * HB * (n - 1) + HB)
                    for h in range(HB):
                        if d == B_ and ahead(b, k):
                            acc = pu[:, h // 2, h % 2, :]
                        else:
                            acc = py[:, h, :]
                            if d == F_ and h < 2:
                                pe.wait_ge(w_ready, 1 + TB * n - 1 + h)
                            elif d == F_:
                                pe.wait_ge(t_squared, 1 + TB * n - 3 + h)
                            else:
                                pe.wait_ge(y_read, 2 * HB * n + h + 1)
                        for c in range(2):
                            states = (st_f[:, c, :] if d == F_ else
                                      st_b[:, bass.ds(slot(b - 1, k), 1), c, :].rearrange("p o t -> p (o t)"))
                            mm = nc.tensor.matmul(acc, ct[:, 2 * d + c, P * h:P * h + P], states,
                                                  start=(c == 0), stop=(c == 1))
                        mm.then_inc(y_done, 1)

            def feed_forward(b, k):
                n = chunk_b(b, k)
                pe.wait_ge(y_read, 2 * HB * (n + 1))
                pe.wait_ge(s_added, 1 + 2 * HB * (n + 1))
                if k == 0:
                    pe.wait_ge(wc_ready, HB)

                def transpose(t):
                    if t >= 2:
                        pe.wait_ge(t_squared, 1 + TB * n + t - 1)
                    for h in range(HB):
                        mm = nc.tensor.transpose(py[:, 2 + t % 2, P * h:P * h + P], s[:, h, P * t:P * t + P],
                                                 ident[:, :])
                    mm.then_inc(t_done, 1)

                def high(t):
                    if t >= 2:
                        pe.wait_ge(w_ready, 1 + TB * n + t - 1)
                    for h in range(HB):
                        nc.tensor.matmul(py[:, t % 2, :], s_hi[:, h, P * t:P * t + P], wc[:, h, :],
                                         start=(h == 0), stop=False)

                def low(t):
                    for h in range(HB):
                        if t == 0:
                            pe.wait_ge(s_lo_ready, HB * n + h + 1)
                        mm = nc.tensor.matmul(py[:, t % 2, :], s_lo[:, h, P * t:P * t + P], wc[:, h, :],
                                              start=False, stop=(h == HB - 1))
                    mm.then_inc(ff_done, 1)

                transpose(0)
                pe.wait_ge(s_hi_ready, HB * (n + 1))
                high(0)
                transpose(1)
                high(1)
                low(0)
                low(1)
                for t in range(2, TB):
                    transpose(t)
                    high(t)
                    low(t)

            def mean_setup():
                pe.wait_ge(abs_sums, 1)
                pe.wait_ge(over_h_ready, 1)
                nc.tensor.matmul(pu[:, 1, 1, 0:1], over_h[:, :], abs_sum[:, :], start=True, stop=True)\
                  .then_inc(mean_abs, 1)

            def row_means_setup():
                pe.wait_ge(ternary_ready, 1)
                pe.wait_ge(in_products, 2 * (NK - 1) + 1)
                for h in range(HB):
                    mm = nc.tensor.matmul(py[:, 1, :], over_h[:, :], ternary[:, h, :],
                                          start=(h == 0), stop=(h == HB - 1))
                mm.then_inc(row_means, 1)

            def step(b, k):
                if first(b):
                    u_products(b, k)
                elif last(b):
                    y_products(b, k, [F_] if ahead(b, k) else [F_, B_])
                    if ahead(b, k + 1):
                        y_products(b, k + 1, [B_])
                elif k == 0:
                    y_products(b, k, [F_])
                    u_products(b, k, [F_])
                    y_products(b, k, [B_])
                    u_products(b, k, [B_])
                elif k < NK - 1:
                    y_products(b, k)
                    u_products(b, k)
                else:
                    u_products(b, k, [F_])
                    y_products(b, k)
                    u_products(b, k, [B_])
                if not first(b):
                    feed_forward(b, k)
                if first(b) and k == 0:
                    mean_setup()
                if first(b) and k == NK - 1:
                    row_means_setup()
                    pe.wait_ge(means_copied, 1)
                    pe.wait_ge(ct_ready, 1)
                    pe.wait_ge(ident_ready, 2)

            steps(pe, step)

        @block.scalar
        def _(act):
            start(act, t_squared, stored)

            act.wait_ge(theta_ready, 1)
            nc.scalar.activation(first_sin[:, :], first_phase[:, 0, :], ACT.Sin)
            nc.scalar.activation(first_cos, first_phase[:, 1, :], ACT.Sin, scale=-1.0).then_inc(first_sincos, 1)
            act.wait_ge(bt_loaded, 16)
            nc.scalar.activation(bt_hi[:, :, :, :], bt_raw, ACT.Copy).then_inc(bt_hi_ready, 1)

            def tables_setup():
                for d in (F_, B_):
                    act.wait_ge(phase_ready, d + 1)
                    nc.scalar.activation(tab_out[:, d, 1, :], phase[:, d, 0, :], ACT.Sin)
                    nc.scalar.activation(tab_out[:, d, 0, :], phase[:, d, 1, :], ACT.Sin, scale=-1.0)\
                      .then_inc(sincos_ready, 1)
                    if d == F_:
                        act.wait_ge(gain_ready, 1)
                    act.wait_ge(sincos_ready, d + 1)
                    sine = tab_out[:, d, 1, :]
                    nc.scalar.activation(phase[:, d, 0, :], sine, ACT.Identity, scale=gain[:, 2 + d:3 + d])
                    nc.scalar.activation(phase[:, d, 1, :], sine, ACT.Identity, scale=gain[:, d:d + 1])\
                      .then_inc(table_products, 1)

            def weights_setup():
                act.wait_ge(wt_loaded, 16)
                nc.scalar.activation(ternary, wt_raw, ACT.Abs, accum_out=abs_sum[:, :]).then_inc(abs_sums, 1)
                act.wait_ge(out_weights_loaded, 32)
                for c in (1, 3):
                    neg = nc.scalar.activation(ct[:, c, :], ct[:, c, :], ACT.Copy, scale=-1.0)
                neg.then_inc(ct_ready, 1)

            def x_high(b, k):
                if not (first(b) and k < 2):
                    act.wait_ge(u_done, 2 * (chunk_a(b, k) - 1))
                act.wait_ge(xa_loaded, 16 * (chunk_a(b, k) + 1))
                for h in range(HB):
                    nc.scalar.activation(x_hi[:, k % 2, h, :], x_a[:, h, :], ACT.Copy).then_inc(x_hi_ready, 1)

            def final(b, k):
                n = chunk_b(b, k)
                act.wait_ge(shift_ready, n + 1)
                halves = 2 if last(b) and k == NK - 1 else 1
                rows = TB // halves
                for i in range(halves):
                    ts = range(rows * i, rows * (i + 1))
                    for t in ts:
                        fin = nc.scalar.activation(w[:, t, :], w[:, t, :], ACT.Identity,
                                                   bias=shift[:, t:t + 1], scale=rstd[:, t:t + 1])
                    fin.then_inc(final_ready, 1)
                    act.wait_ge(final_ready, n + 1 + i)
                    act.dma_start(out_d[bass.ds(n, 1), P * ts[0]:P * (ts[-1] + 1), :]
                                  .rearrange("o (t p) h -> p (o t) h", p=P), w[:, ts[0]:ts[-1] + 1, :])\
                       .then_inc(stored, 16)

            x_high(0, 0)

            def step(b, k):
                if first(b) and k == 0:
                    tables_setup()
                if not first(b):
                    n = chunk_b(b, k)

                    def s_high(h):
                        act.wait_ge(s_added, 1 + 2 * HB * n + HB + h + 1)
                        nc.scalar.activation(s_hi[:, h, :], s[:, h, :], ACT.Copy).then_inc(s_hi_ready, 1)

                    def gelu(n, j):
                        act.wait_ge(y_read, 2 * HB * n + j + 1)
                        nc.scalar.activation(y[:, j, :], y[:, j, :], ACT.Gelu).then_inc(gelu_ready, 1)

                    before_output = 6 if last(b) else 0 if k == NK - 1 else 2
                    here, early = outputs(b, k)
                    for j in here:
                        if k and j == before_output:
                            final(b, k - 1)
                        gelu(n, j)
                        if j >= HB + 2:
                            s_high(j - HB - 2)
                    s_high(HB - 2)
                    s_high(HB - 1)
                if not last(b):
                    x_high(*following(b, k))
                if first(b) and k == 0:
                    weights_setup()
                if first(b) and k == NK - 1:
                    act.wait_ge(row_means, 1)
                    nc.scalar.activation(means, py[:, 1, :], ACT.Copy).then_inc(means_copied, 1)
                if not first(b):
                    for t in range(TB):
                        act.wait_ge(t_done, TB * n + t + 1)
                        act.wait_ge(w_ready, 1 + TB * n + max(t - 1, 0))
                        bank = py[:, 2 + t % 2, :]
                        nc.scalar.activation(s_t[:, t % 2, :], bank, ACT.Copy,
                                             accum_out=sums[:, 0, t:t + 1]).then_inc(t_copied, 1)
                        act.wait_ge(t_copied, TB * n + t + 1)
                        nc.scalar.activation(bank, bank, ACT.Square,
                                             accum_out=sums[:, 1, t:t + 1]).then_inc(t_squared, 1)
                    for j in early:
                        gelu(n + 1, j)
                    if k == NK - 1:
                        final(b, k)

            steps(act, step)

        @block.gpsimd
        def _(pool):
            start(pool, s_added)

            count = [0]

            def link(ins):
                count[0] += 1
                ins.then_inc(pool_step, 1)
                pool.wait_ge(pool_step, count[0])

            nc.gpsimd.memset(minus_half[:, :], -0.5)
            link(nc.gpsimd.memset(e_const[:, :], float(np.e)))
            pool.wait_ge(par_loaded, 16)
            nc.gpsimd.tensor_tensor(exps[:, :], e_const[:, :], log_re_delta, ALU.pow).then_inc(exps_ready, 1)
            nc.gpsimd.memset(over_h[:, :], 1.0 / H).then_inc(over_h_ready, 1)
            nc.gpsimd.memset(ident[:, :], 0.0).then_inc(ident_ready, 1)
            pool.wait_ge(ident_ready, 1)
            nc.gpsimd.affine_select(out=ident[:, :], in_=ident[:, :], compare_op=ALU.not_equal, fill=1.0,
                                    base=0, pattern=[[-1, P]], channel_multiplier=1).then_inc(ident_ready, 1)

            def tt(out, a, b_, op):
                link(nc.gpsimd.tensor_tensor(out, a, b_, op))

            def ts(out, a, s1, s2, op1, op2=None):
                link(nc.gpsimd.tensor_scalar(out, a, s1, s2, op1, op2) if op2 else
                     nc.gpsimd.tensor_scalar(out, a, s1, s2, op1))

            def modulus_setup():
                pool.wait_ge(exps_ready, 1)
                tt(lam_re, minus_re, minus_re, ALU.mult)
                tt(is_small, lambda_im, lambda_im, ALU.mult)
                tt(is_small, is_small, lam_re, ALU.add)
                ts(is_small, is_small, LAM_MIN ** 2, None, ALU.is_lt)
                ts(keep, is_small, -1.0, 1.0, ALU.mult, ALU.add)
                ts(is_small, is_small, LAM_MIN, None, ALU.mult)
                tt(lam_re, minus_re, keep, ALU.mult)
                tt(lam_re, is_small, lam_re, ALU.subtract)
                tt(lam_im, lambda_im, keep, ALU.mult)
                tt(modulus, lam_re, lam_re, ALU.mult)
                tt(temp, lam_im, lam_im, ALU.mult)
                nc.gpsimd.tensor_tensor(modulus, modulus, temp, ALU.add).then_inc(modulus_ready, 1)

            def gain_setup():
                pool.wait_ge(first_sincos, 1)
                pool.wait_ge(decay_ready, 1)
                tt(lr, first_cos, rho[:, :], ALU.mult)
                tt(li, first_sin[:, :], rho[:, :], ALU.mult)
                ts(lr, lr, -1.0, None, ALU.add)
                tt(gain[:, 0:2], lr, lam_re, ALU.mult)
                tt(temp, li, lam_im, ALU.mult)
                tt(gain[:, 0:2], gain[:, 0:2], temp, ALU.add)
                tt(gain[:, 2:4], li, lam_re, ALU.mult)
                tt(temp, lr, lam_im, ALU.mult)
                tt(gain[:, 2:4], gain[:, 2:4], temp, ALU.subtract)
                pool.wait_ge(inverse_ready, 1)
                nc.gpsimd.tensor_tensor(gain[:, 0:2], gain[:, 0:2], modulus, ALU.mult)
                nc.gpsimd.tensor_tensor(gain[:, 2:4], gain[:, 2:4], modulus, ALU.mult).then_inc(gain_ready, 1)

            modulus_setup()
            pool.wait_ge(exponent_ready, 1)
            nc.gpsimd.tensor_tensor(rho[:, :], e_const[:, 0:2], exponent, ALU.pow).then_inc(decay_ready, 1)

            def weights_low(d):
                pool.wait_ge(bt_hi_ready, 1)
                c = slice(2 * d, 2 * d + 2)
                nc.gpsimd.tensor_tensor(bt_lo[:, :, c, :], bt_raw[:, :, c, :], bt_hi[:, :, c, :].bitcast(f32),
                                        ALU.subtract).then_inc(bt_lo_ready, 1)

            def ternary_setup():
                pool.wait_ge(thresholds, 1)
                link(nc.gpsimd.tensor_scalar(ternary, wt_raw, half_scale[:, :], None, ALU.is_gt))

            def ternary_end():
                link(nc.gpsimd.tensor_scalar(wt_raw, wt_raw, minus_half_scale[:, :], None, ALU.is_lt))
                nc.gpsimd.tensor_tensor(ternary, ternary, wt_raw, ALU.subtract).then_inc(ternary_ready, 1)

            def centre_setup():
                pool.wait_ge(means_copied, 1)
                for h in range(HB):
                    nc.gpsimd.tensor_tensor(wc[:, h, :], ternary[:, h, :], means, ALU.subtract)\
                      .then_inc(wc_ready, 1)

            def x_low(b, k):
                for h in range(HB):
                    pool.wait_ge(x_hi_ready, HB * chunk_a(b, k) + h + 1)
                    nc.gpsimd.tensor_tensor(x_lo[:, k % 2, h, :], x_a[:, h, :], x_hi[:, k % 2, h, :].bitcast(f32),
                                            ALU.subtract)\
                      .then_inc(x_lo_ready, 1)

            def norm_factors(b, k):
                n = chunk_b(b, k)
                pool.wait_ge(var_ready, n + 1)
                nc.gpsimd.tensor_tensor(rstd[:, :], var_e[:, :], minus_half[:, :], ALU.pow).then_inc(rstd_ready, 1)
                pool.wait_ge(rstd_ready, n + 1)
                nc.gpsimd.tensor_tensor(shift[:, :], neg_mean[:, :], rstd[:, :], ALU.mult).then_inc(shift_ready, 1)

            weights_low(F_)
            gain_setup()
            x_low(0, 0)
            weights_low(B_)

            def step(b, k):
                if not first(b):
                    here, early = outputs(b, k)
                    if k and not last(b):
                        norm_factors(b, k - 1)
                    n = chunk_b(b, k)

                    def s_low(h):
                        pool.wait_ge(s_hi_ready, HB * n + h + 1)
                        nc.gpsimd.tensor_tensor(s_lo[:, h, :], s[:, h, :], s_hi[:, h, :].bitcast(f32),
                                                ALU.subtract).then_inc(s_lo_ready, 1)

                    def add(n, j):
                        h = j % HB
                        if j == 0:
                            pool.wait_ge(xb_loaded, 16 * (n + 1))
                            pool.wait_ge(ff_done, 1 + TB * n)
                        pool.wait_ge(gelu_ready, 2 * HB * n + j + 1)
                        if j >= HB:
                            pool.wait_ge(s_added, 1 + 2 * HB * n + h + 1)
                        nc.gpsimd.tensor_tensor(s[:, h, :], (x_b if j < HB else s)[:, h, :], y[:, j, :],
                                                ALU.add).then_inc(s_added, 1)

                    for j in here:
                        add(n, j)
                    for h in range(HB):
                        s_low(h)
                if not last(b):
                    x_low(*following(b, k))
                if first(b) and k == NK - 1:
                    centre_setup()
                if first(b) and k == 1:
                    ternary_setup()
                if first(b) and k == 2:
                    ternary_end()
                if not first(b):
                    for j in early[:2]:
                        add(n + 1, j)
                    if k == NK - 1 or last(b):
                        norm_factors(b, k)
                    for j in early[2:]:
                        add(n + 1, j)

            steps(pool, step)

        @block.vector
        def _(dve):
            start(dve, w_ready)

            count = [0]

            def link(ins):
                count[0] += 1
                ins.then_inc(setup_step, 1)
                dve.wait_ge(setup_step, count[0])

            V = nc.vector

            def tables_setup():
                jv = z
                link(V.memset(st_f[:, 0, :], 1.0))
                link(V.tensor_tensor_scan(jv[:, 0, :], st_f[:, 0, :], st_f[:, 0, :], 0.0, ALU.mult, ALU.add))
                link(V.tensor_copy(jv[:, 1, ::-1], jv[:, 0, :]))
                dve.wait_ge(exps_ready, 1)
                link(V.scalar_tensor_tensor(out=exponent, in0=minus_re, scalar=-1.0, in1=delta,
                                            op0=ALU.mult, op1=ALU.mult))
                V.tensor_tensor(theta, lambda_im, delta, ALU.mult).then_inc(exponent_ready, 1)
                dve.wait_ge(exponent_ready, 1)
                link(V.tensor_scalar(turns, theta, 1 / TWO_PI, MAGIC, ALU.mult, ALU.add))
                link(V.tensor_scalar(turns, turns, MAGIC, None, ALU.subtract))
                for part in (PI_1, PI_2, PI_3):
                    link(V.scalar_tensor_tensor(out=theta, in0=turns, scalar=-part, in1=theta,
                                                op0=ALU.mult, op1=ALU.add))
                phase_1, minus_cophase_1 = first_phase[:, 0, :], first_phase[:, 1, :]
                link(V.tensor_scalar(phase_1, theta, PI_DOWN, -PI_DOWN, ALU.min, ALU.max))
                link(V.scalar_tensor_tensor(out=minus_cophase_1, in0=phase_1, scalar=-1.0, in1=phase_1,
                                            op0=ALU.mult, op1=ALU.max))
                V.tensor_scalar(minus_cophase_1, minus_cophase_1, float(np.pi / 2), None, ALU.subtract)\
                 .then_inc(theta_ready, 1)
                link(V.tensor_copy(th_hi[:, :], theta))
                link(V.tensor_tensor(th_lo, theta, th_hi[:, :].bitcast(f32), ALU.subtract))
                for d in (F_, B_):
                    ph, q = phase[:, d, 0, :], phase[:, d, 1, :]
                    link(V.tensor_scalar(ph, jv[:, d, :], th_hi[:, d:d + 1].bitcast(f32), None, ALU.mult))
                    link(V.tensor_scalar(q, jv[:, d, :], theta[:, d:d + 1], 1 / TWO_PI, ALU.mult, ALU.mult))
                    link(V.tensor_scalar(q, q, MAGIC, MAGIC, ALU.add, ALU.subtract))
                    link(V.scalar_tensor_tensor(out=ph, in0=q, scalar=-PI_1, in1=ph, op0=ALU.mult, op1=ALU.add))
                    link(V.scalar_tensor_tensor(out=ph, in0=q, scalar=-PI_2, in1=ph, op0=ALU.mult, op1=ALU.add))
                    link(V.scalar_tensor_tensor(out=ph, in0=jv[:, d, :], scalar=th_lo[:, d:d + 1], in1=ph,
                                                op0=ALU.mult, op1=ALU.add))
                    link(V.tensor_scalar(ph, ph, PI_DOWN, -PI_DOWN, ALU.min, ALU.max))
                    link(V.scalar_tensor_tensor(out=q, in0=ph, scalar=-1.0, in1=ph, op0=ALU.mult, op1=ALU.max))
                    V.tensor_scalar(q, q, float(np.pi / 2), None, ALU.subtract).then_inc(phase_ready, 1)
                    if d == F_:
                        dve.wait_ge(modulus_ready, 1)
                        V.reciprocal(modulus, modulus).then_inc(inverse_ready, 1)

            def tab_in_setup(d):
                dve.wait_ge(table_products, d + 1)
                if d == F_:
                    dve.wait_ge(gain_ready, 1)
                cos = tab_out[:, d, 0, :]
                V.scalar_tensor_tensor(out=tab_in[:, d, 0, :], in0=cos, scalar=gain[:, d:d + 1],
                                       in1=phase[:, d, 0, :], op0=ALU.mult, op1=ALU.add)
                link(V.scalar_tensor_tensor(out=tab_in[:, d, 1, :], in0=cos, scalar=gain[:, 2 + d:3 + d],
                                            in1=phase[:, d, 1, :], op0=ALU.mult, op1=ALU.subtract))

            def ternary_setup():
                dve.wait_ge(mean_abs, 1)
                link(V.tensor_scalar(scale[:, :], pu[:, 1, 1, 0:1], 1.0 / H, EPS, ALU.mult, ALU.max))
                link(V.tensor_scalar(half_scale[:, :], scale[:, :], 0.5, None, ALU.mult))
                V.tensor_scalar(minus_half_scale[:, :], scale[:, :], -0.5, None, ALU.mult).then_inc(thresholds, 1)

            def wide(table):
                return table.to_broadcast([P, 2, T])

            def rotate_in(b, k, d, done):
                rotate_in_products(b, k, d, done)
                rotate_in_sums(b, k, d)

            def rotate_in_products(b, k, d, done):
                n = 2 * chunk_a(b, k) + d
                dve.wait_ge(rotated, done)
                dve.wait_ge(u_done, n + 1)
                u = u_banks(b, k)[:, d, :, :]
                V.tensor_tensor(prod[:, 0, :, :], u, wide(tab_in[:, d, 0:1, :]), ALU.mult)
                V.tensor_tensor(u, u, wide(tab_in[:, d, 1:2, :]), ALU.mult)\
                 .then_inc(in_products, 1)

            def rotate_in_sums(b, k, d):
                dve.wait_ge(in_products, 2 * chunk_a(b, k) + d + 1)
                u = u_banks(b, k)[:, d, :, :]
                if d == F_:
                    sl = bass.ds(slot(b, NK - 1 - k), 1)
                    re, im = (v_f[:, sl, c, :].rearrange("p o t -> p (o t)") for c in range(2))
                else:
                    im, re = u[:, 0, :], u[:, 1, :]
                V.tensor_tensor(re, prod[:, 0, 0, :], u[:, 1, :], ALU.subtract)
                V.tensor_tensor(im, prod[:, 0, 1, :], u[:, 0, :], ALU.add).then_inc(rotated, 1)

            def scan_b(b, k, c, done):
                dve.wait_ge(rotated, done)
                if k == 0:
                    init = 0.0
                else:
                    init = st_b[:, bass.ds(slot(b, NK - k), 1), c, 0:1].rearrange("p o t -> p (o t)")
                v = u_banks(b, k)[:, B_, 1 - c, ::-1]
                op = V.tensor_tensor_scan(v, rho[:, B_:B_ + 1].to_broadcast([P, T]), v, init, ALU.mult, ALU.add)
                if c:
                    op.then_inc(zb_ready, 1)

            def out_b(b, k):
                sl = bass.ds(slot(b, NK - 1 - k), 1)
                re, im = (st_b[:, sl, c, :].rearrange("p o t -> p (o t)") for c in range(2))
                if not first(b):
                    dve.wait_ge(y_done, 1 + 2 * HB * (chunk_b(b, k) + 1))
                n = chunk_a(b, k)
                dve.wait_ge(zb_ready, n + 1)
                u = u_banks(b, k)[:, B_, :, :]
                V.tensor_tensor(prod[:, 0, :, :], u, wide(tab_out[:, B_, 0:1, :]), ALU.mult)
                V.tensor_tensor(u, u, wide(tab_out[:, B_, 1:2, :]), ALU.mult).then_inc(outb_products, 1)
                dve.wait_ge(outb_products, n + 1)
                V.tensor_tensor(re, prod[:, 0, 1, :], u[:, 0, :], ALU.subtract)
                V.tensor_tensor(im, prod[:, 0, 0, :], u[:, 1, :], ALU.add).then_inc(rotated, 1)

            def scan_f(b, k, c, done):
                dve.wait_ge(rotated, done)
                if k == 0:
                    init = 0.0
                else:
                    init = st_f[:, c, T - 1:T]
                sl = bass.ds(slot(b - 1, k), 1)
                op = V.tensor_tensor_scan(z[:, c, :], rho[:, F_:F_ + 1].to_broadcast([P, T]),
                                          v_f[:, sl, c, :].rearrange("p o t -> p (o t)"), init, ALU.mult, ALU.add)
                if c:
                    op.then_inc(zf_ready, 1)

            def out_f(b, k):
                n = chunk_b(b, k)
                dve.wait_ge(zf_ready, n + 1)
                V.tensor_tensor(prod[:, 0, :, :], z[:, :, :], wide(tab_out[:, F_, 0:1, :]), ALU.mult)
                V.tensor_tensor(prod[:, 1, :, :], z[:, :, :], wide(tab_out[:, F_, 1:2, :]), ALU.mult)\
                 .then_inc(outf_products, 1)
                dve.wait_ge(outf_products, n + 1)
                V.tensor_tensor(st_f[:, 0, :], prod[:, 0, 0, :], prod[:, 1, 1, :], ALU.subtract)
                V.tensor_tensor(st_f[:, 1, :], prod[:, 0, 1, :], prod[:, 1, 0, :], ALU.add).then_inc(rotated, 1)

            def read_y(b, k, j):
                n = chunk_b(b, k)
                half, h = divmod(j, HB)
                d = 1 - half if ahead(b, k) else half
                bank = pu[:, h // 2, h % 2, :] if ahead(b, k) and d == B_ else py[:, h, :]
                if j == 0:
                    dve.wait_ge(xb_loaded, 16 * (n + 1))
                if k:
                    dve.wait_ge(s_added, 1 + 2 * HB * n - (2 * HB - 1 - j))
                elif j == 0:
                    dve.wait_ge(s_added, 1 + 2 * HB * n)
                dve.wait_ge(y_done, 1 + 2 * HB * n + j + 1)
                V.scalar_tensor_tensor(out=y[:, j, :], in0=x_b[:, h, :], scalar=d_sb[:, d, h:h + 1],
                                       in1=bank, op0=ALU.mult, op1=ALU.add).then_inc(y_read, 1)

            def result(b, k, t):
                n = chunk_b(b, k)
                if t == 0:
                    dve.wait_ge(stored, 16 + 16 * n)
                dve.wait_ge(t_copied, TB * n + t + 1)
                dve.wait_ge(ff_done, 1 + TB * n + t + 1)
                V.scalar_tensor_tensor(out=w[:, t, :], in0=py[:, t % 2, :], scalar=scale[:, 0:1],
                                       in1=s_t[:, t % 2, :], op0=ALU.mult, op1=ALU.add).then_inc(w_ready, 1)

            def moments(b, k, t):
                n = chunk_b(b, k)
                dve.wait_ge(w_ready, 1 + TB * n + t + 1)
                V.bn_stats(stats[:, t, :], w[:, t, :]).then_inc(stats_ready, 1)

            def variances(b, k):
                n = chunk_b(b, k)
                dve.wait_ge(stats_ready, TB * (n + 1))
                dve.wait_ge(t_squared, 1 + TB * (n + 1))
                V.tensor_tensor(mean_gap[:, :], stats[:, :, 1], stats[:, :, 4], ALU.subtract)
                V.tensor_tensor(mean_sum[:, :], stats[:, :, 1], stats[:, :, 4], ALU.add).then_inc(halves_read, 1)
                V.tensor_tensor(sq_sum[:, :], stats[:, :, 2], stats[:, :, 5], ALU.add)
                V.scalar_tensor_tensor(out=var_s[:, :], in0=sums[:, 0, :], scalar=-1 / H, in1=sums[:, 0, :],
                                       op0=ALU.mult, op1=ALU.mult)
                dve.wait_ge(halves_read, n + 1)
                V.scalar_tensor_tensor(out=var_w[:, :], in0=mean_gap[:, :], scalar=H / 4, in1=mean_gap[:, :],
                                       op0=ALU.mult, op1=ALU.mult).then_inc(gap_squared, 1)
                V.tensor_scalar(neg_mean[:, :], mean_sum[:, :], -0.5, None, ALU.mult)
                dve.wait_ge(gap_squared, n + 1)
                V.tensor_tensor(var_w[:, :], var_w[:, :], sq_sum[:, :], ALU.add)
                V.tensor_tensor(var_s[:, :], var_s[:, :], sums[:, 1, :], ALU.add).then_inc(vars_ready, 1)
                dve.wait_ge(vars_ready, n + 1)
                V.scalar_tensor_tensor(out=var_e[:, :], in0=var_s[:, :], scalar=EPS, in1=var_w[:, :],
                                       op0=ALU.mult, op1=ALU.add).then_inc(eps_added, 1)
                dve.wait_ge(eps_added, n + 1)
                V.tensor_scalar(var_e[:, :], var_e[:, :], 1 / H, EPS * EPS, ALU.mult, ALU.add).then_inc(var_ready, 1)

            def backward(b, k, done):
                scan_b(b, k, 0, done)
                scan_b(b, k, 1, done)
                out_b(b, k)

            def forward(b, k, done):
                scan_f(b, k, 0, done)
                scan_f(b, k, 1, done)
                out_f(b, k)

            def norm(b, k):
                for t in range(TB):
                    result(b, k, t)
                    moments(b, k, t)
                variances(b, k)

            def first_sequence(k, done):
                if k:
                    backward(0, k - 1, done)
                    done += 1
                rotate_in(0, k, F_, done)
                if k == 0:
                    tab_in_setup(B_)
                if k < NK - 1:
                    rotate_in(0, k, B_, done + 1)
                else:
                    forward(1, 0, done + 1)
                    rotate_in(0, k, B_, done + 2)
                    backward(0, k, done + 3)
                if k == 0:
                    ternary_setup()

            def first_chunk(b, done):
                for j in range(HB):
                    read_y(b, 0, j)
                rotate_in_products(b, 0, F_, done)
                read_y(b, 0, HB)
                read_y(b, 0, HB + 1)
                rotate_in_sums(b, 0, F_)
                for j in range(HB + 2, 2 * HB):
                    read_y(b, 0, j)
                forward(b, 1, done + 1)
                rotate_in(b, 0, B_, done + 2)
                norm(b, 0)

            def middle_chunk(b, k, done):
                read_y(b, k, 0)
                scan_b(b, k - 1, 0, done)
                read_y(b, k, 1)
                scan_b(b, k - 1, 1, done)
                read_y(b, k, 2)
                out_b(b, k - 1)
                for j in range(3, 2 * HB):
                    read_y(b, k, j)
                forward(b, k + 1, done + 1)
                rotate_in(b, k, F_, done + 2)
                rotate_in(b, k, B_, done + 3)
                norm(b, k)

            def last_chunk(b, done):
                k = NK - 1
                backward(b, k - 1, done)
                read_y(b, k, 0)
                rotate_in(b, k, F_, done + 1)
                for j in range(1, 2 * HB):
                    read_y(b, k, j)
                forward(b + 1, 0, done + 2)
                rotate_in(b, k, B_, done + 3)
                for c in range(2):
                    result(b, k, c)
                    moments(b, k, c)
                    scan_b(b, k, c, done + 4)
                result(b, k, 2)
                moments(b, k, 2)
                result(b, k, 3)
                moments(b, k, 3)
                variances(b, k)
                out_b(b, k)

            def last_sequence(k, done):
                here, early = outputs(NB, k)
                for j in here:
                    read_y(NB, k, j)
                if k < NK - 1:
                    forward(NB, k + 1, done)
                for j in early:
                    read_y(NB, k + 1, j)
                norm(NB, k)

            def step(b, k):
                done = rotations(b, k)
                if first(b):
                    first_sequence(k, done)
                elif last(b):
                    last_sequence(k, done)
                elif k == 0:
                    first_chunk(b, done)
                elif k < NK - 1:
                    middle_chunk(b, k, done)
                else:
                    last_chunk(b, done)

            tables_setup()
            tab_in_setup(F_)
            steps(dve, step)


def kernel(**inputs):
    import numpy as _np
    import concourse.bacc as _bacc
    from concourse import mybir as _mybir
    from concourse.bass_utils import run_bass_kernel_spmd as _run

    a = {n.removeprefix("L0_").removeprefix("attn_"): _np.asarray(v) for n, v in inputs.items()}
    arrays = {
        "x": a["x"].reshape(NB * NK, T, HB, P).transpose(0, 3, 2, 1),
        "bt": _np.stack([a[f"{d}_B_{c}"].T.reshape(HB, P, P) for d in ("fwd", "bwd")
                         for c in ("real", "imag")], 2).transpose(1, 0, 2, 3),
        "ct": _np.stack([a[f"{d}_C_{c}"].T for d in ("fwd", "bwd") for c in ("real", "imag")], 1),
        "wt": a["ffn_weight"].T.reshape(HB, P, H).transpose(1, 0, 2),
        "d": _np.stack([a["fwd_D"].reshape(HB, P).T, a["bwd_D"].reshape(HB, P).T], 1),
        "par": _np.stack([a["fwd_log_real"], a["bwd_log_real"], a["fwd_log_Delta"], a["bwd_log_Delta"],
                          a["fwd_imag"], a["bwd_imag"]], 1),
    }
    arrays = {n: _np.ascontiguousarray(v) for n, v in arrays.items()}
    nc = _bacc.Bacc("TRN2", target_bir_lowering=False, num_devices=1)
    args = [nc.dram_tensor(f"{n}_dram", v.shape, _mybir.dt.from_np(v.dtype), kind="ExternalInput").ap()
            for n, v in arrays.items()]
    out = nc.dram_tensor("out_dram", (NB * NK, T, H), _mybir.dt.float32, kind="ExternalOutput").ap()
    build(nc, *args, out)
    r = _run(nc, [{f"{n}_dram": v for n, v in arrays.items()}], core_ids=[0])
    return r.results[0]["out_dram"].reshape(NB, L, H)
```
